# Optimizing a Trainium2 kernel written in Bass

```python
import numpy as np
import jax
import jax.numpy as jnp

def _softmax(x, axis=-1):
    return jax.nn.softmax(x, axis=axis)

def _gelu(x):
    return jax.nn.gelu(x, approximate=True)

def _silu(x):
    return jax.nn.silu(x)

def _sigmoid(x):
    return jax.nn.sigmoid(x)

def _layernorm(x, axis=-1, eps=1e-05):
    m = jnp.mean(x, axis=axis, keepdims=True)
    v = jnp.var(x, axis=axis, keepdims=True)
    return (x - m) / jnp.sqrt(v + eps)

def _scatter_add(tgt, idx, src, axis=0):
    return tgt.at[idx].add(src)

def _segment_sum(src, seg, n):
    return jax.ops.segment_sum(src, seg, n)
kernel_name = 'mk_decoder_preln_d1_seqx_r4_b60331'

def setup_inputs(seed: int=0):
    np.random.seed(seed)
    _w = jnp.asarray

    def _rec_inputs():
        import jax
        import jax.numpy as jnp
        _rk = jax.random.key(seed)
        x = -0.000125 + 0.9999 * jax.random.normal(jax.random.fold_in(_rk, 1), (4, 512, 512), jnp.float32)
        _lenS = 512 - jax.random.randint(jax.random.fold_in(_rk, 7), (4,), 0, max(1, 512 // 4) + 1, jnp.int32)
        _lenS2 = 64 - jax.random.randint(jax.random.fold_in(_rk, 8), (4,), 0, max(1, 64 // 4) + 1, jnp.int32)
        _ctx_2048P = jax.random.normal(jax.random.fold_in(_rk, 11), (4, 16, 512), jnp.float32)
        _ctx_2048c = jax.random.dirichlet(jax.random.fold_in(_rk, 511), 0.3 * jnp.ones((16,), jnp.float32), (4, 64))
        _ctx_2048t = jnp.einsum('bsk,bkd->bsd', _ctx_2048c, _ctx_2048P)
        _ctx_2048t = _ctx_2048t * jax.lax.rsqrt(jnp.mean(jnp.square(_ctx_2048t)) + 1e-12) * 0.953939
        ctx_2048 = -0.000514642 + 1.00011 * (_ctx_2048t + 0.3 * jax.random.normal(jax.random.fold_in(_rk, 611), (4, 64, 512), jnp.float32))
        _validS = jnp.arange(512)[None, :] < _lenS[:, None]
        _validS2 = jnp.arange(64)[None, :] < _lenS2[:, None]
        _causal = jnp.tril(jnp.ones((512, 512), dtype=bool))
        mask_BxS2_bk0 = jnp.logical_not(jnp.broadcast_to(_validS2[:, :], (4, 64)))
        return (x, ctx_2048, mask_BxS2_bk0)
    x, ctx_2048, mask_BxS2_bk0 = _rec_inputs()

    def _L0_attn_setup():
        import jax, jax.numpy as jnp
        import numpy as np
        B, S, H_DIM = (2, 512, 512)
        N_HEADS, D_HEAD = (16, 128)
        key = jax.random.key(seed)
        k1, k2, k3 = jax.random.split(key, 3)
        x = jax.random.normal(k1, (B, S, H_DIM), dtype=jnp.float32)
        w_qkv = jax.random.normal(k2, (H_DIM, 3 * N_HEADS * D_HEAD), dtype=jnp.float32) * 0.02
        w_o = jax.random.normal(k3, (N_HEADS * D_HEAD, H_DIM), dtype=jnp.float32) * 0.02
        return {'x': x, 'w_qkv': w_qkv, 'w_o': w_o}
    _L0_attn_all = _L0_attn_setup()
    _L0_attn_in = {k: v for k, v in _L0_attn_all.items() if k in ('w_qkv', 'w_o')}
    del _L0_attn_all

    def _L0_xattn_setup():
        import jax, jax.numpy as jnp
        import numpy as np
        key = jax.random.key(seed)
        k1, k2, k3 = jax.random.split(key, 3)
        B, S, D, M = (8, 512, 512, 128)
        hidden_states = jax.random.normal(k1, (B, S, D), dtype=jnp.float32)
        memory_tokens = jax.random.normal(k2, (B, M, D), dtype=jnp.float32)
        memory_mask = jax.random.randint(k3, (B, M), 0, 2).astype(jnp.bool_)
        return {'hidden_states': hidden_states, 'memory_tokens': memory_tokens, 'memory_mask': memory_mask}
    _L0_xattn_all = _L0_xattn_setup()
    _L0_xattn_in = {k: v for k, v in _L0_xattn_all.items() if k in ()}
    del _L0_xattn_all

    def _L0_ffn_setup():
        import jax, jax.numpy as jnp
        import numpy as np
        D_IN = 512
        D_OUT = 512
        RANK = 16
        N_EXPERTS = 16
        MAX_EXPERTS = 32
        ROUTER_HID = 64
        TOPK = 2
        ALPHA = 1.0

        def _forward(x, W, bias, rw1, rb1, rw2, rb2, A, B, gates):
            lead = x.shape[:-1]
            x_flat = x.reshape(-1, D_IN)
            n = x_flat.shape[0]
            feat = jax.lax.stop_gradient(x_flat)
            h = jax.nn.silu(feat @ rw1.T + rb1)
            logits = (h @ rw2.T + rb2)[:, :N_EXPERTS] + gates[None, :]
            topv, topi = jax.lax.top_k(logits, TOPK)
            sm = jax.nn.softmax(topv, axis=-1)
            rows = jnp.arange(n)[:, None]
            coeff = jnp.zeros_like(logits).at[rows, topi].set(sm)
            base = x_flat @ W.T + bias
            xa = jnp.einsum('ni,eri->ner', x_flat, A)
            wxa = xa * coeff[:, :, None]
            delta = jnp.einsum('ner,eor->no', wxa, B)
            out = base + ALPHA * delta
            return out.reshape(*lead, D_OUT)
        key = jax.random.key(seed)
        ks = jax.random.split(key, 10)
        s = 0.02
        x = jax.random.normal(ks[0], (4, 1024, D_IN), dtype=jnp.float32)
        W = jax.random.normal(ks[1], (D_OUT, D_IN), dtype=jnp.float32) * s
        bias = jax.random.normal(ks[2], (D_OUT,), dtype=jnp.float32) * s
        rw1 = jax.random.normal(ks[3], (ROUTER_HID, D_IN), dtype=jnp.float32) * s
        rb1 = jnp.zeros((ROUTER_HID,), dtype=jnp.float32)
        rw2 = jax.random.normal(ks[4], (MAX_EXPERTS, ROUTER_HID), dtype=jnp.float32) * s
        rb2 = jnp.zeros((MAX_EXPERTS,), dtype=jnp.float32)
        A = jax.random.normal(ks[5], (N_EXPERTS, RANK, D_IN), dtype=jnp.float32) * s
        B = jax.random.normal(ks[6], (N_EXPERTS, D_OUT, RANK), dtype=jnp.float32) * s
        gates = jnp.ones((N_EXPERTS,), dtype=jnp.float32)
        return {'x': x, 'W': W, 'bias': bias, 'rw1': rw1, 'rb1': rb1, 'rw2': rw2, 'rb2': rb2, 'A': A, 'B': B, 'gates': gates}
    _L0_ffn_all = _L0_ffn_setup()
    _L0_ffn_in = {k: v for k, v in _L0_ffn_all.items() if k in ('W', 'bias', 'rw1', 'rb1', 'rw2', 'rb2', 'A', 'B', 'gates')}
    del _L0_ffn_all
    return {'x': x, 'ctx_2048': ctx_2048, 'mask_BxS2_bk0': mask_BxS2_bk0, 'L0_attn_w_qkv': _L0_attn_in['w_qkv'], 'L0_attn_w_o': _L0_attn_in['w_o'], 'L0_ffn_W': _L0_ffn_in['W'], 'L0_ffn_bias': _L0_ffn_in['bias'], 'L0_ffn_rw1': _L0_ffn_in['rw1'], 'L0_ffn_rb1': _L0_ffn_in['rb1'], 'L0_ffn_rw2': _L0_ffn_in['rw2'], 'L0_ffn_rb2': _L0_ffn_in['rb2'], 'L0_ffn_A': _L0_ffn_in['A'], 'L0_ffn_B': _L0_ffn_in['B'], 'L0_ffn_gates': _L0_ffn_in['gates']}

def reference(x, ctx_2048, mask_BxS2_bk0, L0_attn_w_qkv, L0_attn_w_o, L0_ffn_W, L0_ffn_bias, L0_ffn_rw1, L0_ffn_rb1, L0_ffn_rw2, L0_ffn_rb2, L0_ffn_A, L0_ffn_B, L0_ffn_gates):
    import jax
    import jax.numpy as jnp

    def _L0_attn_ref(x, w_qkv, w_o):
        import jax, jax.numpy as jnp
        import numpy as np
        B, S, H_DIM = (2, 512, 512)
        N_HEADS, D_HEAD = (16, 128)
        b, s, _ = x.shape
        qkv = jnp.einsum('bsh,hf->bsf', x, w_qkv)
        qkv = qkv.reshape(b, s, 3, N_HEADS, D_HEAD)
        q, k, v = (qkv[:, :, 0], qkv[:, :, 1], qkv[:, :, 2])
        q = q.transpose(0, 2, 1, 3)
        k = k.transpose(0, 2, 1, 3)
        v = v.transpose(0, 2, 1, 3)
        scores = jnp.einsum('bhqd,bhkd->bhqk', q, k) / jnp.sqrt(jnp.float32(D_HEAD))
        probs = jax.nn.softmax(scores, axis=-1)
        values = jnp.einsum('bhqk,bhkd->bhkd', probs, v)
        values = values.transpose(0, 2, 1, 3).reshape(b, s, N_HEADS * D_HEAD)
        out = jnp.einsum('bsf,fh->bsh', values, w_o)
        return out

    def _L0_xattn_ref(hidden_states, memory_tokens, memory_mask):
        import jax, jax.numpy as jnp
        import numpy as np
        B, S, D = hidden_states.shape
        scale = 1.0 / jnp.sqrt(jnp.asarray(D, hidden_states.dtype))
        scores = jnp.einsum('bsd,bmd->bsm', hidden_states, memory_tokens) * scale
        neg_inf = jnp.asarray(-1e+30, scores.dtype)
        scores = jnp.where(memory_mask[:, None, :], scores, neg_inf)
        attn = jax.nn.softmax(scores, axis=-1)
        readout = jnp.einsum('bsm,bmd->bsd', attn, memory_tokens)
        valid_b = jnp.any(memory_mask, axis=-1)
        out = jnp.where(valid_b[:, None, None], readout, jnp.zeros_like(readout))
        return out

    def _L0_ffn_ref(x, W, bias, rw1, rb1, rw2, rb2, A, B, gates):
        import jax, jax.numpy as jnp
        import numpy as np
        D_IN = 512
        D_OUT = 512
        RANK = 16
        N_EXPERTS = 16
        MAX_EXPERTS = 32
        ROUTER_HID = 64
        TOPK = 2
        ALPHA = 1.0

        def _forward(x, W, bias, rw1, rb1, rw2, rb2, A, B, gates):
            lead = x.shape[:-1]
            x_flat = x.reshape(-1, D_IN)
            n = x_flat.shape[0]
            feat = jax.lax.stop_gradient(x_flat)
            h = jax.nn.silu(feat @ rw1.T + rb1)
            logits = (h @ rw2.T + rb2)[:, :N_EXPERTS] + gates[None, :]
            topv, topi = jax.lax.top_k(logits, TOPK)
            sm = jax.nn.softmax(topv, axis=-1)
            rows = jnp.arange(n)[:, None]
            coeff = jnp.zeros_like(logits).at[rows, topi].set(sm)
            base = x_flat @ W.T + bias
            xa = jnp.einsum('ni,eri->ner', x_flat, A)
            wxa = xa * coeff[:, :, None]
            delta = jnp.einsum('ner,eor->no', wxa, B)
            out = base + ALPHA * delta
            return out.reshape(*lead, D_OUT)
        return _forward(x, W, bias, rw1, rb1, rw2, rb2, A, B, gates)
    x = x + _L0_attn_ref(_layernorm(x, axis=-1), L0_attn_w_qkv, L0_attn_w_o)
    x = x + _L0_xattn_ref(_layernorm(x, axis=-1), ctx_2048, mask_BxS2_bk0)
    x = x + _L0_ffn_ref(_layernorm(x, axis=-1), L0_ffn_W, L0_ffn_bias, L0_ffn_rw1, L0_ffn_rb1, L0_ffn_rw2, L0_ffn_rb2, L0_ffn_A, L0_ffn_B, L0_ffn_gates)
    return x

_drawn_inputs = setup_inputs


def setup_inputs(seed=0):
    import zlib

    import numpy as np

    out = dict(_drawn_inputs(seed))
    spreads = {'L0_ffn_rb1': (0.0, 0.8), 'L0_ffn_rb2': (0.0, 0.8), 'L0_ffn_gates': (1.0, 0.6)}
    factors = {'L0_ffn_bias': 3.947,
     'L0_ffn_rw1': 8.0,
     'L0_ffn_rw2': 8.0,
     'L0_ffn_A': 3.03,
     'L0_ffn_B': 3.107}
    for name, (base, spread) in spreads.items():
        noise = np.random.default_rng([zlib.crc32(name.encode()), seed]).standard_normal(out[name].shape)
        drawn = base * np.exp(spread * noise) if base else spread * noise
        out[name] = jnp.asarray(drawn.astype(out[name].dtype))
    for name, factor in factors.items():
        out[name] = (out[name] * factor).astype(out[name].dtype)
    return out
```

```python
import math
from contextlib import ExitStack

import concourse.bass as bass
from concourse import mybir


def decoder_layer(nc, A_x, A_mem, A_mask, A_wqkv, A_wo, A_W, A_bias, A_rw1, A_rb1, A_rw2, A_rb2,
                  A_A, A_B, A_gates, out):
    fp32 = mybir.dt.float32
    f32r = mybir.dt.float32r
    i32 = mybir.dt.int32
    u32 = mybir.dt.uint32
    ALU = mybir.AluOpType
    ACT = mybir.ActivationFunctionType
    AX = mybir.AxisListType

    P = 128
    NB, SQ, D = A_x.shape
    NT = SQ // P
    NK = D // P
    F = A_wqkv.shape[1] // 3
    DH = P
    NH = F // DH
    NPAIR = NH // 2
    SLOTS = 2 * NB
    NSLOT = NPAIR * SLOTS
    M = A_mem.shape[1]
    NE, RANK = A_A.shape[0], A_A.shape[1]
    ER = NE * RANK
    NA = ER // P
    RH = A_rw1.shape[0]
    XW = ER + RH
    SCALE = 1.0 / math.sqrt(DH)
    MSCALE = 1.0 / math.sqrt(D)
    EPS = 1e-5
    NEG = 1e30
    HI, LO = 0, 1

    x_view = A_x.rearrange("b (t p) d -> p b t d", p=P)
    out_view = out.rearrange("b (t p) d -> p b t d", p=P)
    wqkv_view = A_wqkv.rearrange("(k p) (c n d) -> n c p k d", p=P, c=3, d=DH)
    wo_view = A_wo.rearrange("(q j d) n -> q d j n", j=2, d=DH)

    ctx = ExitStack()
    with ctx:
        def sb(name, shape, dt=fp32):
            return ctx.enter_context(nc.sbuf_tensor(name, shape, dt))

        def sem(name):
            return ctx.enter_context(nc.semaphore(name))

        x_res = sb("x_res", [P, NB, NT, D])
        ident = sb("ident", [P, P])
        big = sb("big", [P, 2 * NK * NB * SQ], f32r)
        xT = big[:, :].rearrange("p (h k n) -> p h k n", h=2, k=NK)
        wsp = sb("wsp", [P, 2, 2, NK, 3 * DH], f32r)
        wstage = sb("wstage", [P, (NK * 3 * DH + 2 * D)])
        wq_raw = wstage[:, 0:NK * 3 * DH].rearrange("p (k c d) -> p k c d", k=NK, c=3)
        wo_raw = wstage[:, NK * 3 * DH:].rearrange("p (j n) -> p j n", j=2)
        wosp = sb("wosp", [P, 2, 2, D], f32r)
        qk = sb("qk", [P, 2, 2, 2, SQ], f32r)
        work = sb("work", [P, 4, SQ])
        v_sb = work[:, 0:2, :]
        acc = work[:, 2, :]
        val = work[:, 3, :]
        E = sb("E", [P, NT, SQ])
        accsp = sb("accsp", [P, 2, SQ], f32r)
        ones = sb("ones", [P, P], f32r)
        val0 = sb("val0", [P, NB, 2, SQ], f32r)
        val1 = sb("val1", [P, 2, 2, SQ], f32r)
        negm = sb("negm", [P, 2, NT])
        zsum = sb("zsum", [P, 2, NT])
        rz = sb("rz", [P, 2, NT])
        bn = sb("bn", [P, NT, 6])
        mv = sb("mv", [P, NT, 2])
        va = sb("va", [P, NT])
        yi = sb("yi", [P, 2, NT])
        yt = sb("yt", [P, NT])
        maskb = sb("maskb", [P, NB, M], A_mask.dtype)
        maskf = sb("maskf", [P, NB, M])
        pen = sb("pen", [P, NB, M])
        valid = sb("valid", [P, NB])
        memT = sb("memT", [P, NB, NK, M])
        sc = sb("sc", [P, NT, M])
        es = sb("es", [P, NT, M])
        mnegm = sb("mnegm", [P, NT])
        mz = sb("mz", [P, NT])
        mrz = sb("mrz", [P, NT])
        biasb = sb("biasb", [P, D])
        rb1b = sb("rb1b", [P, RH])
        rbgb = sb("rbgb", [P, NE])
        gateb = sb("gateb", [P, NE])
        rw2_raw = sb("rw2_raw", [NE, RH])
        rw2T = sb("rw2T", [RH, NE])
        rw1_raw = sb("rw1_raw", [RH, D])
        iot = sb("iot", [P, NE])
        z = sb("z", [P, NT, RH])
        ez = sb("ez", [P, NT, RH])
        lg = sb("lg", [P, NT, NE])
        top = sb("top", [P, NT, 8])
        topi = sb("topi", [P, NT, 8], u32)
        topf = sb("topf", [P, NT, 2])
        dd = sb("dd", [P, NT])
        p1 = sb("p1", [P, NT])
        p2 = sb("p2", [P, NT])
        cf = sb("cf", [P, 2, NT, NE])

        cut = [0]

        def part(n):
            a = big[:, cut[0]:cut[0] + n]
            cut[0] += n
            return a

        WT = part(2 * NK * D).rearrange("p (h k n) -> p h k n", h=2, k=NK)
        XAW = part(2 * NK * XW).rearrange("p (h k n) -> p h k n", h=2, k=NK)
        BT = part(2 * NA * D).rearrange("p (h a n) -> p h a n", h=2, a=NA)
        x2T = part(2 * NK * SQ).rearrange("p (h k n) -> p h k n", h=2, k=NK)
        wxT = part(2 * 2 * NA * P).rearrange("p (s h a n) -> p s h a n", s=2, h=2, a=NA)
        W_raw = E
        A_raw = work[:, 0:2, :]
        B_raw = work[:, 2:4, :].rearrange("p a (b n) -> p (a b) n", b=2)
        x1T = work[:, 0:2, :].rearrange("p s (k n) -> p s k n", k=NK)
        hT = work[0:RH, 2, :]
        eT = work[0:M, 3, :]
        mem_raw = wstage[0:M, 0:NB * D].rearrange("p (b d) -> p b d", b=NB)
        wxa = wstage[:, NB * D:NB * D + 2 * ER].rearrange("p (s n) -> p s n", s=2)

        proj = [ctx.enter_context(nc.psum_tensor(f"proj{i}", [P, SQ], fp32)) for i in range(2)]
        sps = [ctx.enter_context(nc.psum_tensor(f"score{i}", [P, SQ], fp32)) for i in range(NT)]
        colp = ctx.enter_context(nc.psum_tensor("colp", [P, SQ], fp32))
        outp = ctx.enter_context(nc.psum_tensor("outp", [P, SQ], fp32))
        Y = [colp, outp]

        x_loaded = [sem(f"x_loaded{b}") for b in range(NB)]
        w_loaded = sem("w_loaded")
        wo_loaded = sem("wo_loaded")
        small_loaded = sem("small_loaded")
        mem_loaded = sem("mem_loaded")
        tail_loaded = sem("tail_loaded")
        stored = sem("stored")
        ident_ready = sem("ident_ready")
        ones_ready = sem("ones_ready")
        dve_chain = sem("dve_chain")
        pool_chain = sem("pool_chain")
        xn_ready = sem("xn_ready")
        xtr_done = sem("xtr_done")
        xhi_ready = sem("xhi_ready")
        xlo_ready = sem("xlo_ready")
        w_hi = sem("w_hi")
        w_split = sem("w_split")
        wo_hi = sem("wo_hi")
        wo_split = sem("wo_split")
        q_proj = sem("q_proj")
        k_proj = sem("k_proj")
        v_proj = sem("v_proj")
        q_hi = sem("q_hi")
        k_hi = sem("k_hi")
        q_split = sem("q_split")
        k_split = sem("k_split")
        v_copied = sem("v_copied")
        s_done = sem("s_done")
        max_ready = sem("max_ready")
        e_ready = sem("e_ready")
        rz_ready = sem("rz_ready")
        acc_step = sem("acc_step")
        acc_hi = sem("acc_hi")
        acc_split = sem("acc_split")
        c_done = sem("c_done")
        val_ready = sem("val_ready")
        val_hi = sem("val_hi")
        val_split = sem("val_split")
        o_done = sem("o_done")
        o_added = sem("o_added")
        prep_done = sem("prep_done")
        prep_hi = sem("prep_hi")
        prep_ready = sem("prep_ready")
        memT_ready = sem("memT_ready")
        x1_ready = sem("x1_ready")
        ms_done = sem("ms_done")
        ms_masked = sem("ms_masked")
        ms_max = sem("ms_max")
        es_ready = sem("es_ready")
        etr_done = sem("etr_done")
        eT_ready = sem("eT_ready")
        read_done = sem("read_done")
        x2_ready = sem("x2_ready")
        xa_done = sem("xa_done")
        z_ready = sem("z_ready")
        ez_ready = sem("ez_ready")
        h_ready = sem("h_ready")
        htr_done = sem("htr_done")
        hT_ready = sem("hT_ready")
        lg_done = sem("lg_done")
        lg_ready = sem("lg_ready")
        dd_ready = sem("dd_ready")
        ed_ready = sem("ed_ready")
        wxa_ready = sem("wxa_ready")
        wtr_done = sem("wtr_done")
        wx_hi = sem("wx_hi")
        wx_ready = sem("wx_ready")
        biased = sem("biased")
        y_mm = sem("y_mm")
        y_ready = sem("y_ready")

        def wait(eng, semaphore, value):
            if not isinstance(value, int) or value > 0:
                eng.wait_ge(semaphore, value)

        def is_first(p):
            return isinstance(p, int) and p == 0

        def is_last(p):
            return isinstance(p, int) and p == NPAIR - 1

        def pairs(eng, body):
            body(0)
            with eng.Fori(1, NPAIR - 1) as p:
                body(p)
            body(NPAIR - 1)

        TAIL = [("x", 0), ("x", 1), ("f", 0), ("x", 2), ("f", 1), ("x", 3), ("f", 2), ("f", 3)]
        NPREP = NK + NK + NA

        block = ctx.enter_context(nc.Block())

        @block.sync
        def _(sp):
            def load_w(h):
                for c in range(3):
                    sp.dma_start(wq_raw[:, :, c, :], wqkv_view[h, c]).then_inc(w_loaded, 16)

            sp.dma_start(x_res[:, 0], x_view[:, 0]).then_inc(x_loaded[0], 16)
            load_w(0)
            for b in range(1, NB):
                sp.dma_start(x_res[:, b], x_view[:, b]).then_inc(x_loaded[b], 16)
            sp.dma_start(maskb[:, :, :], A_mask.partition_broadcast(P)).then_inc(small_loaded, 16)
            sp.dma_start(biasb[:, :], A_bias.partition_broadcast(P)).then_inc(small_loaded, 16)
            sp.dma_start(rb1b[:, :], A_rb1.partition_broadcast(P)).then_inc(small_loaded, 16)
            sp.dma_start(rbgb[:, :], A_rb2[0:NE].partition_broadcast(P)).then_inc(small_loaded, 16)
            sp.dma_start(gateb[:, :], A_gates.partition_broadcast(P)).then_inc(small_loaded, 16)
            sp.dma_start(rw2_raw[:, :], A_rw2[0:NE, :]).then_inc(small_loaded, 16)
            sp.dma_start(rw1_raw[:, :], A_rw1).then_inc(small_loaded, 16)

            def pair(p):
                sp.wait_ge(w_split, p * 2 + 1)
                load_w(p * 2 + 1)
                wait(sp, wo_split, p)
                sp.dma_start(wo_raw, wo_view[p]).then_inc(wo_loaded, 16)
                if not is_last(p):
                    sp.wait_ge(w_split, p * 2 + 2)
                    load_w(p * 2 + 2)

            pairs(sp, pair)
            sp.wait_ge(w_split, NH)
            sp.wait_ge(wo_split, NPAIR)
            sp.dma_start(mem_raw, A_mem.rearrange("b m d -> m b d")).then_inc(mem_loaded, 16)
            sp.wait_ge(acc_step, NT * NSLOT)
            sp.dma_start(W_raw[:, :, :], A_W.rearrange("(t p) i -> p t i", p=P)).then_inc(tail_loaded, 16)
            sp.wait_ge(val_split, NSLOT)
            sp.dma_start(A_raw, A_A.rearrange("e r i -> (e r) i").rearrange("(a p) i -> p a i", p=P))\
                .then_inc(tail_loaded, 16)
            b_view = A_B.rearrange("e (t p) r -> t p e r", p=P)
            for t in range(D // P):
                sp.dma_start(B_raw[:, t, :].rearrange("p (e r) -> p e r", r=RANK), b_view[t])\
                    .then_inc(tail_loaded, 16)
            for b in range(NB):
                sp.wait_ge(y_ready, NT * (b + 1))
                sp.dma_start(out_view[:, b], x_res[:, b]).then_inc(stored, 16)
            sp.wait_ge(stored, 16 * NB)

        @block.gpsimd
        def _(pool):
            chain = [0]

            def link(ins):
                chain[0] += 1
                ins.then_inc(pool_chain, 1)
                pool.wait_ge(pool_chain, chain[0])

            link(nc.gpsimd.memset(ident[:, :], 0.0))
            nc.gpsimd.affine_select(out=ident[:, :], in_=ident[:, :], compare_op=ALU.not_equal, fill=1.0,
                                    base=0, pattern=[[-1, P]], channel_multiplier=1).then_inc(ident_ready, 1)
            nc.gpsimd.memset(ones[:, :].bitcast(fp32), 1.0).then_inc(ones_ready, 1)
            pool.wait_ge(ones_ready, 1)
            link(nc.gpsimd.iota(iot[:, :], pattern=[[1, NE]], base=0, channel_multiplier=0,
                                allow_small_or_imprecise_dtypes=True))

            def high(dst, src):
                one = ones[:, 0:1].bitcast(fp32).to_broadcast([P, src.shape[1]])
                return nc.gpsimd.tensor_tensor(dst, src, one, ALU.mult)

            def split_w(h, parity):
                pool.wait_ge(w_loaded, h * 48 + 48)
                raw = wstage[:, 0:NK * 3 * DH]
                hi, lo = (wsp[:, parity, f].rearrange("p k n -> p (k n)") for f in (HI, LO))
                high(hi, raw).then_inc(w_hi, 1)
                pool.wait_ge(w_hi, h + 1)
                nc.gpsimd.tensor_tensor(lo, raw, hi.bitcast(fp32), ALU.subtract).then_inc(w_split, 1)

            def slot(p, j):
                n1 = p * SLOTS + j
                if not (is_first(p) and j == 0):
                    b, head = (j - 1) % NB, (j - 1) // NB % 2
                    pool.wait_ge(acc_step, n1 * NT)
                    wait(pool, c_done, n1 - 1)
                    high(accsp[:, HI], acc).then_inc(acc_hi, 1)
                    pool.wait_ge(acc_hi, n1)
                    nc.gpsimd.tensor_tensor(accsp[:, LO], acc, accsp[:, HI].bitcast(fp32),
                                            ALU.subtract).then_inc(acc_split, 1)
                    pool.wait_ge(val_ready, n1)
                    if head == 0 or j == 0:
                        dst = val0[:, b] if head == 0 else val1[:, b % 2]
                    else:
                        dst = val1[:, b % 2]
                    if head == 0:
                        wait(pool, o_done, p * (NB * NT) + (b + 1 - NB) * NT)
                    elif j == 0:
                        wait(pool, o_done, p * (NB * NT) + (b - 1 - NB) * NT)
                    else:
                        wait(pool, o_done, p * (NB * NT) + (b - 1) * NT)
                    high(dst[:, HI], val).then_inc(val_hi, 1)
                    pool.wait_ge(val_hi, n1)
                    nc.gpsimd.tensor_tensor(dst[:, LO], val, dst[:, HI].bitcast(fp32),
                                            ALU.subtract).then_inc(val_split, 1)
                if j == 1 or (j == 1 + NB and not is_last(p)):
                    h = p * 2 + (1 if j == 1 else 2)
                    wait(pool, v_proj, h * NB - NB)
                    split_w(h, 1 if j == 1 else 0)
                if j == 3:
                    pool.wait_ge(wo_loaded, p * 16 + 16)
                    wait(pool, o_done, p * (NB * NT))
                    raw = wstage[:, NK * 3 * DH:]
                    hi, lo = (wosp[:, f].rearrange("p j n -> p (j n)") for f in (HI, LO))
                    high(hi, raw).then_inc(wo_hi, 1)
                    pool.wait_ge(wo_hi, p + 1)
                    nc.gpsimd.tensor_tensor(lo, raw, hi.bitcast(fp32), ALU.subtract).then_inc(wo_split, 1)

            def pair(p):
                for j in range(SLOTS):
                    slot(p, j)

            split_w(0, 0)
            pairs(pool, pair)
            slot(NPAIR, 0)
            for i, (kind, b) in enumerate(TAIL):
                if kind == "f":
                    if i == 2:
                        pool.wait_ge(small_loaded, 7 * 16)
                    pool.wait_ge(xn_ready, NT * (NB + i + 1))
                    for t in range(NT):
                        nc.gpsimd.tensor_tensor(x_res[:, b, t], x_res[:, b, t], biasb[:, :], ALU.add)\
                            .then_inc(biased, 1)

        @block.tensor
        def _(pe):
            def halves(out_ap, lhsT, rhs, start, stop):
                nc.tensor.matmul(out_ap, lhsT(HI), rhs(HI), start=start, stop=False)
                nc.tensor.matmul(out_ap, lhsT(HI), rhs(LO), start=False, stop=False)
                return nc.tensor.matmul(out_ap, lhsT(LO), rhs(HI), start=False, stop=stop)

            pe.wait_ge(ident_ready, 1)
            for b in range(NB):
                for t in range(NT):
                    pe.wait_ge(xn_ready, b * NT + t + 1)
                    wait(pe, xlo_ready, (b - 1) * NT + t + 1)
                    for k in range(NK):
                        mm = nc.tensor.transpose(sps[t][:, k * P:(k + 1) * P], E[:, t, k * P:(k + 1) * P],
                                                 ident[:, :])
                    mm.then_inc(xtr_done, 1)

            def project(c, b, parity, bank):
                for k in range(NK):
                    mm = halves(proj[bank][:, :],
                                lambda f: wsp[:, parity, f, k, c * DH:(c + 1) * DH],
                                lambda f: xT[:, f, k, b * SQ:(b + 1) * SQ], k == 0, k == NK - 1)
                return mm

            def q_project(p, j, n):
                b, head = j % NB, j // NB % 2
                if b == 0:
                    pe.wait_ge(w_split, p * 2 + (j // NB) + 1)
                wait(pe, k_split, n)
                project(0, b, head, (n_parity(j - 1) * 3) % 2).then_inc(q_proj, 1)

            def n_parity(j):
                return j % 2

            def k_project(p, j, n):
                wait(pe, v_copied, n - 1)
                project(1, j % NB, j // NB % 2, (n_parity(j - 1) * 3 + 1) % 2).then_inc(k_proj, 1)

            def v_project(p, j, n, has_next):
                if has_next:
                    pe.wait_ge(q_split, n + 2)
                project(2, j % NB, j // NB % 2, (n_parity(j) * 3 + 2) % 2).then_inc(v_proj, 1)

            def scores(j, n, t):
                if t == 0:
                    pe.wait_ge(q_split, n + 1)
                    pe.wait_ge(k_split, n + 1)
                wait(pe, e_ready, n * NT + (t + 1 - NT))
                halves(sps[t][:, :], lambda f: qk[:, j % 2, 0, f, t * P:(t + 1) * P],
                       lambda f: qk[:, j % 2, 1, f, :], True, True).then_inc(s_done, 1)

            def column_sums(n):
                pe.wait_ge(acc_split, n)
                wait(pe, val_ready, n - 1)
                nc.tensor.matmul(colp[:, :], ones[:, :], accsp[:, HI], start=True, stop=False)
                nc.tensor.matmul(colp[:, :], ones[:, :], accsp[:, LO], start=False, stop=True)\
                    .then_inc(c_done, 1)

            def out_tile(p, b, t):
                if t == 0:
                    pe.wait_ge(val_split, p * SLOTS + NB + b + 1)
                    if b == 0:
                        pe.wait_ge(wo_split, p + 1)
                wait(pe, o_added, p * (NB * NT) + b * NT + t)
                halves(outp[:, :], lambda f: val0[:, b, f, t * P:(t + 1) * P],
                       lambda f: wosp[:, f, 0, :], True, False)
                halves(outp[:, :], lambda f: val1[:, b % 2, f, t * P:(t + 1) * P],
                       lambda f: wosp[:, f, 1, :], False, True).then_inc(o_done, 1)

            def slot(p, j):
                n = p * SLOTS + j
                has_next = not (is_last(p) and j == SLOTS - 1)
                outs = []
                if j >= NB + 2:
                    outs = [(p, j - 2 - NB, t) for t in range(NT)]
                elif j < 2 and not is_first(p):
                    outs = [(p - 1, j + NB - 2, t) for t in range(NT)]

                def some(k):
                    if outs:
                        out_tile(*outs[k])

                if has_next:
                    q_project(p, j + 1, n + 1)
                some(0)
                scores(j, n, 0)
                scores(j, n, 1)
                some(1)
                if has_next:
                    k_project(p, j + 1, n + 1)
                if not (is_first(p) and j == 0):
                    column_sums(n)
                some(2)
                scores(j, n, 2)
                scores(j, n, 3)
                v_project(p, j, n, has_next)
                some(3)

            def pair(p):
                for j in range(SLOTS):
                    slot(p, j)

            pe.wait_ge(ones_ready, 1)
            pe.wait_ge(xlo_ready, NB * NT)
            q_project(0, 0, 0)
            k_project(0, 0, 0)
            pairs(pe, pair)
            column_sums(NSLOT)
            for b in (NB - 2, NB - 1):
                for t in range(NT):
                    out_tile(NPAIR - 1, b, t)

            turn = [0]
            release = [(k_split, NSLOT), (v_copied, NSLOT)]

            def take(done_sem, done_value):
                i = turn[0] % 2
                if turn[0] < 2:
                    pe.wait_ge(k_split, NSLOT)
                    pe.wait_ge(v_copied, NSLOT)
                else:
                    pe.wait_ge(*release[i])
                release[i] = (done_sem, done_value)
                turn[0] += 1
                return proj[i]

            pe.wait_ge(tail_loaded, 16 * 6)
            pe.wait_ge(small_loaded, 16 * 7)
            for k in range(NK):
                bank = take(prep_ready, k + 1)
                for t in range(D // P):
                    mm = nc.tensor.transpose(bank[:, t * P:(t + 1) * P], W_raw[:, t, k * P:(k + 1) * P],
                                             ident[:, :])
                mm.then_inc(prep_done, 1)
            for k in range(NK):
                bank = take(prep_ready, NK + k + 1)
                for a in range(NA):
                    nc.tensor.transpose(bank[:, a * P:(a + 1) * P], A_raw[:, a, k * P:(k + 1) * P],
                                        ident[:, :])
                nc.tensor.matmul(bank[:, ER:XW], rw1_raw[:, k * P:(k + 1) * P], ident[0:RH, 0:RH],
                                 start=True, stop=True).then_inc(prep_done, 1)
            for a in range(NA):
                bank = take(prep_ready, 2 * NK + a + 1)
                for t in range(D // P):
                    mm = nc.tensor.transpose(bank[:, t * P:(t + 1) * P], B_raw[:, t, a * P:(a + 1) * P],
                                             ident[:, :])
                mm.then_inc(prep_done, 1)
            bank = take(prep_ready, NPREP + 1)
            nc.tensor.matmul(bank[0:RH, 0:NE], rw2_raw[:, :], ident[0:NE, 0:NE], start=True, stop=True)\
                .then_inc(prep_done, 1)
            pe.wait_ge(mem_loaded, 16)
            for b in range(NB):
                bank = take(memT_ready, b + 1)
                for k in range(NK):
                    mm = nc.tensor.matmul(bank[:, k * M:(k + 1) * M], mem_raw[:, b, k * P:(k + 1) * P],
                                          ident[0:M, 0:M], start=True, stop=True)
                mm.then_inc(prep_done, 1)

            def turned(u, t, done_sem, done_value):
                pe.wait_ge(xn_ready, u * NT + t + 1)
                bank = take(done_sem, done_value)
                for k in range(NK):
                    mm = nc.tensor.transpose(bank[:, k * P:(k + 1) * P], E[:, t, k * P:(k + 1) * P],
                                             ident[:, :])
                mm.then_inc(xtr_done, 1)

            def memory(u, b):
                banks = {}
                score_bank = None
                for t in range(NT + 1):
                    if t < NT:
                        turned(u, t, x1_ready, b * NT + t + 1)
                    if t == 1:
                        wait(pe, ms_masked, b)
                    if t >= 1:
                        pe.wait_ge(x1_ready, b * NT + t)
                        for k in range(NK):
                            mm = nc.tensor.matmul(ms_bank(t - 1), x1T[:, (t - 1) % 2, k, :],
                                                  memT[:, b, k, :], start=(k == 0), stop=(k == NK - 1))
                        mm.then_inc(ms_done, 1)
                pe.wait_ge(es_ready, (b + 1) * NT)
                bank = take(eT_ready, b + 1)
                for t in range(NT):
                    mm = nc.tensor.matmul(bank[0:M, t * P:(t + 1) * P], es[:, t, :], ident[:, :],
                                          start=True, stop=True)
                mm.then_inc(etr_done, 1)
                pe.wait_ge(eT_ready, b + 1)
                for t in range(NT):
                    bank = take(x2_ready, b * NT + t + 1)
                    nc.tensor.matmul(bank[:, :], eT[:, t * P:(t + 1) * P], mem_raw[:, b, :],
                                     start=True, stop=True).then_inc(read_done, 1)

            def ms_bank(t):
                return outp[:, t * M:(t + 1) * M]

            def experts(u, b):
                for t in range(NT):
                    turned(u, t, xlo_ready, NB * NT + b * NT + t + 1)
                for t in range(NT):
                    pe.wait_ge(xlo_ready, NB * NT + b * NT + t + 1)
                    wait(pe, wxa_ready, (b - 1) * NT + t + 1)
                    for k in range(NK):
                        mm = halves(sps[t][:, 0:XW], lambda f: x2T[:, f, k, t * P:(t + 1) * P],
                                    lambda f: XAW[:, f, k, :], k == 0, k == NK - 1)
                    mm.then_inc(xa_done, 1)
                bank = take(hT_ready, b + 1)
                pe.wait_ge(h_ready, b + 1)
                for t in range(NT):
                    mm = nc.tensor.matmul(bank[0:RH, t * P:(t + 1) * P], z[:, t, :], ident[:, :],
                                          start=True, stop=True)
                mm.then_inc(htr_done, 1)
                bank = take(lg_ready, b + 1)
                pe.wait_ge(hT_ready, b + 1)
                for t in range(NT):
                    mm = nc.tensor.matmul(bank[:, t * NE:(t + 1) * NE], hT[:, t * P:(t + 1) * P],
                                          rw2T[:, :], start=True, stop=True)
                mm.then_inc(lg_done, 1)
                for t in range(NT):
                    wait(pe, y_ready, b * NT + t)
                    for k in range(NK):
                        halves(colp[:, :], lambda f: x2T[:, f, k, t * P:(t + 1) * P],
                               lambda f: WT[:, f, k, :], k == 0, False)
                    pe.wait_ge(wxa_ready, b * NT + t + 1)
                    bank = take(wx_ready, b * NT + t + 1)
                    for a in range(NA):
                        mm = nc.tensor.transpose(bank[:, a * P:(a + 1) * P],
                                                 wxa[:, t % 2, a * P:(a + 1) * P], ident[:, :])
                    mm.then_inc(wtr_done, 1)
                    pe.wait_ge(wx_ready, b * NT + t + 1)
                    for a in range(NA):
                        mm = halves(colp[:, :], lambda f: wxT[:, t % 2, f, a, :],
                                    lambda f: BT[:, f, a, :], False, a == NA - 1)
                    mm.then_inc(y_mm, 1)

            pe.wait_ge(o_added, NPAIR * NB * NT)
            for i, (kind, b) in enumerate(TAIL):
                (memory if kind == "x" else experts)(NB + i, b)

        @block.scalar
        def _(act):
            for b in range(NB):
                for t in range(NT):
                    act.wait_ge(xtr_done, b * NT + t + 1)
                    nc.scalar.activation(xT[:, HI, :, (b * NT + t) * P:(b * NT + t + 1) * P],
                                         sps[t][:, :].rearrange("p (k n) -> p k n", k=NK), ACT.Copy)\
                        .then_inc(xhi_ready, 1)

            def q_high(j, n):
                act.wait_ge(q_proj, n + 1)
                wait(act, s_done, n * NT - NT)
                nc.scalar.activation(qk[:, j % 2, 0, HI], proj[((j - 1) % 2 * 3) % 2][:, :], ACT.Copy,
                                     scale=SCALE).then_inc(q_hi, 1)

            def k_high(j, n):
                act.wait_ge(k_proj, n + 1)
                nc.scalar.activation(qk[:, j % 2, 1, HI], proj[((j - 1) % 2 * 3 + 1) % 2][:, :], ACT.Copy)\
                    .then_inc(k_hi, 1)

            def exponentials(j, n, t):
                act.wait_ge(max_ready, n * NT + t + 1)
                wait(act, acc_step, n * NT + (t + 1 - NT))
                nc.scalar.activation(E[:, t, :], sps[t][:, :], ACT.Exp, bias=negm[:, j % 2, t:t + 1],
                                     accum_out=zsum[:, j % 2, t:t + 1]).then_inc(e_ready, 1)

            def slot(p, j):
                n = p * SLOTS + j
                has_next = not (is_last(p) and j == SLOTS - 1)
                if has_next:
                    q_high(j + 1, n + 1)
                exponentials(j, n, 0)
                exponentials(j, n, 1)
                if has_next:
                    k_high(j + 1, n + 1)
                exponentials(j, n, 2)
                exponentials(j, n, 3)
                act.wait_ge(v_proj, n + 1)
                wait(act, val_ready, n - 1)
                nc.scalar.activation(v_sb[:, j % 2], proj[(j % 2 * 3 + 2) % 2][:, :], ACT.Copy)\
                    .then_inc(v_copied, 1)

            def pair(p):
                for j in range(SLOTS):
                    slot(p, j)

            q_high(0, 0)
            k_high(0, 0)
            pairs(act, pair)

            turn = [0]

            def bank():
                turn[0] += 1
                return proj[(turn[0] - 1) % 2]

            for i in range(NPREP):
                act.wait_ge(prep_done, i + 1)
                src = bank()
                if i < NK:
                    dst, n = WT[:, HI, i], D
                elif i < 2 * NK:
                    dst, n = XAW[:, HI, i - NK], XW
                else:
                    dst, n = BT[:, HI, i - 2 * NK], D
                nc.scalar.activation(dst, src[:, 0:n], ACT.Copy).then_inc(prep_hi, 1)
            bank()
            for b in range(NB):
                act.wait_ge(prep_done, NPREP + 1 + b + 1)
                nc.scalar.activation(memT[:, b].rearrange("p k m -> p (k m)"), bank()[:, 0:NK * M], ACT.Copy)\
                    .then_inc(memT_ready, 1)

            def memory(u, b):
                for t in range(NT):
                    act.wait_ge(xtr_done, u * NT + t + 1)
                    wait(act, ms_done, b * NT + t - 1)
                    nc.scalar.activation(x1T[:, t % 2], bank()[:, :].rearrange("p (k n) -> p k n", k=NK),
                                         ACT.Copy).then_inc(x1_ready, 1)
                for t in range(NT):
                    if t == 0:
                        act.wait_ge(ms_max, b + 1)
                    nc.scalar.activation(es[:, t, :], sc[:, t, :], ACT.Exp, bias=mnegm[:, t:t + 1],
                                         accum_out=mz[:, t:t + 1]).then_inc(es_ready, 1)
                act.wait_ge(etr_done, b + 1)
                nc.scalar.activation(eT, bank()[0:M, :], ACT.Copy).then_inc(eT_ready, 1)
                for t in range(NT):
                    bank()

            def experts(u, b):
                for t in range(NT):
                    act.wait_ge(xtr_done, u * NT + t + 1)
                    wait(act, y_mm, (b - 1) * NT + t + 1)
                    nc.scalar.activation(x2T[:, HI, :, t * P:(t + 1) * P],
                                         bank()[:, :].rearrange("p (k n) -> p k n", k=NK), ACT.Copy)\
                        .then_inc(xhi_ready, 1)
                act.wait_ge(z_ready, b + 1)
                nc.scalar.activation(ez[:, :, :], z[:, :, :], ACT.Exp, scale=-1.0).then_inc(ez_ready, 1)
                act.wait_ge(htr_done, b + 1)
                nc.scalar.activation(hT, bank()[0:RH, :], ACT.Copy).then_inc(hT_ready, 1)
                bank()
                act.wait_ge(dd_ready, b + 1)
                nc.scalar.activation(p2[:, :], dd[:, :], ACT.Exp).then_inc(ed_ready, 1)
                for t in range(NT):
                    act.wait_ge(wtr_done, b * NT + t + 1)
                    wait(act, y_mm, b * NT + t - 1)
                    nc.scalar.activation(wxT[:, t % 2, HI].rearrange("p a n -> p (a n)"),
                                         bank()[:, 0:ER], ACT.Copy).then_inc(wx_hi, 1)

            for i, (kind, b) in enumerate(TAIL):
                (memory if kind == "x" else experts)(NB + i, b)

        @block.vector
        def _(dve):
            chain = [0]

            def link(ins):
                chain[0] += 1
                ins.then_inc(dve_chain, 1)
                dve.wait_ge(dve_chain, chain[0])

            def norm(u, b):
                for t in range(NT):
                    link(nc.vector.bn_stats(bn[:, t], x_res[:, b, t]))
                for t in range(NT):
                    link(nc.vector.bn_aggr(mv[:, t], bn[:, t]))
                y = yi[:, 0]
                link(nc.vector.tensor_scalar(va[:, :], mv[:, :, 1], EPS, None, ALU.add))
                link(nc.vector.tensor_scalar(yi[:, 1].bitcast(i32), va[:, :].bitcast(i32), 1, None,
                                             ALU.logical_shift_right))
                link(nc.vector.tensor_scalar(y.bitcast(i32), yi[:, 1].bitcast(i32), -1.0,
                                             float(0x5F3759DF), ALU.mult, ALU.add))
                for _ in range(3):
                    link(nc.vector.tensor_tensor(yt[:, :], y, y, ALU.mult))
                    link(nc.vector.scalar_tensor_tensor(yt[:, :], yt[:, :], -0.5, va[:, :], ALU.mult, ALU.mult))
                    link(nc.vector.scalar_tensor_tensor(y, yt[:, :], 1.5, y, ALU.add, ALU.mult))
                for t in range(NT):
                    wait(dve, xtr_done, (u - 1) * NT + t + 1)
                    nc.vector.tensor_scalar(E[:, t, :], x_res[:, b, t], mv[:, t, 0:1], y[:, t:t + 1],
                                            ALU.subtract, ALU.mult).then_inc(xn_ready, 1)

            for b in range(NB):
                dve.wait_ge(x_loaded[b], 16)
                norm(b, b)
                for t in range(NT):
                    dve.wait_ge(xhi_ready, b * NT + t + 1)
                    at = slice((b * NT + t) * P, (b * NT + t + 1) * P)
                    nc.vector.tensor_tensor(xT[:, LO, :, at], sps[t][:, :].rearrange("p (k n) -> p k n", k=NK),
                                            xT[:, HI, :, at].bitcast(fp32), ALU.subtract)\
                        .then_inc(xlo_ready, 1)

            def q_low(j, n):
                dve.wait_ge(q_hi, n + 1)
                nc.vector.scalar_tensor_tensor(qk[:, j % 2, 0, LO], proj[((j - 1) % 2 * 3) % 2][:, :], SCALE,
                                               qk[:, j % 2, 0, HI].bitcast(fp32), ALU.mult, ALU.subtract)\
                    .then_inc(q_split, 1)

            def k_low(j, n):
                dve.wait_ge(k_hi, n + 1)
                nc.vector.tensor_tensor(qk[:, j % 2, 1, LO], proj[((j - 1) % 2 * 3 + 1) % 2][:, :],
                                        qk[:, j % 2, 1, HI].bitcast(fp32), ALU.subtract)\
                    .then_inc(k_split, 1)

            def maximum(j, n, t):
                dve.wait_ge(s_done, n * NT + t + 1)
                nc.vector.tensor_reduce(negm[:, j % 2, t:t + 1], sps[t][:, :], AX.X, ALU.max, negate=True)\
                    .then_inc(max_ready, 1)

            def add_out(p, b, t):
                dve.wait_ge(o_done, p * (NB * NT) + b * NT + t + 1)
                nc.vector.tensor_tensor(x_res[:, b, t], x_res[:, b, t], outp[:, :], ALU.add)\
                    .then_inc(o_added, 1)

            def values(j, n):
                dve.wait_ge(c_done, n)
                dve.wait_ge(v_copied, n)
                wait(dve, val_split, n - 1)
                nc.vector.tensor_tensor(val, v_sb[:, (j - 1) % 2], colp[:, :], ALU.mult)\
                    .then_inc(val_ready, 1)

            def sum_queries(j, n):
                dve.wait_ge(e_ready, n * NT + NT)
                nc.vector.reciprocal(rz[:, j % 2], zsum[:, j % 2]).then_inc(rz_ready, 1)
                dve.wait_ge(rz_ready, n + 1)
                wait(dve, acc_split, n)
                for t in range(NT):
                    if t == 0:
                        ins = nc.vector.tensor_scalar(acc, E[:, 0, :], rz[:, j % 2, 0:1], None, ALU.mult)
                    else:
                        dve.wait_ge(acc_step, n * NT + t)
                        ins = nc.vector.scalar_tensor_tensor(acc, E[:, t, :], rz[:, j % 2, t:t + 1], acc,
                                                             ALU.mult, ALU.add)
                    ins.then_inc(acc_step, 1)

            def slot(p, j):
                n = p * SLOTS + j
                has_next = not (is_last(p) and j == SLOTS - 1)
                outs = []
                if j >= NB + 2:
                    outs = [(p, j - 2 - NB, t) for t in range(NT)]
                elif j < 2 and not is_first(p):
                    outs = [(p - 1, j + NB - 2, t) for t in range(NT)]

                def some(k):
                    if outs:
                        add_out(*outs[k])

                if has_next:
                    q_low(j + 1, n + 1)
                some(0)
                maximum(j, n, 0)
                maximum(j, n, 1)
                some(1)
                if has_next:
                    k_low(j + 1, n + 1)
                if not (is_first(p) and j == 0):
                    values(j, n)
                some(2)
                maximum(j, n, 2)
                maximum(j, n, 3)
                some(3)
                sum_queries(j, n)

            def pair(p):
                for j in range(SLOTS):
                    slot(p, j)

            q_low(0, 0)
            k_low(0, 0)
            pairs(dve, pair)
            values(0, NSLOT)
            for b in (NB - 2, NB - 1):
                for t in range(NT):
                    add_out(NPAIR - 1, b, t)

            turn = [0]

            def bank():
                turn[0] += 1
                return proj[(turn[0] - 1) % 2]

            dve.wait_ge(small_loaded, 16 * 7)
            link(nc.vector.tensor_copy(maskf[:, :, :], maskb[:, :, :]))
            link(nc.vector.tensor_scalar(pen[:, :, :], maskf[:, :, :], 1.0, NEG, ALU.subtract, ALU.mult))
            link(nc.vector.tensor_reduce(valid[:, :], maskf[:, :, :], AX.X, ALU.max))
            link(nc.vector.tensor_tensor(rbgb[:, :], rbgb[:, :], gateb[:, :], ALU.add))
            for i in range(NPREP):
                dve.wait_ge(prep_hi, i + 1)
                src = bank()
                if i < NK:
                    dst, n = WT[:, :, i], D
                elif i < 2 * NK:
                    dst, n = XAW[:, :, i - NK], XW
                else:
                    dst, n = BT[:, :, i - 2 * NK], D
                nc.vector.tensor_tensor(dst[:, LO], src[:, 0:n], dst[:, HI].bitcast(fp32), ALU.subtract)\
                    .then_inc(prep_ready, 1)
            dve.wait_ge(prep_done, NPREP + 1)
            nc.vector.tensor_copy(rw2T[:, :], bank()[0:RH, 0:NE]).then_inc(prep_ready, 1)
            for b in range(NB):
                bank()

            def memory(u, b):
                norm(u, b)
                for t in range(NT):
                    bank()
                dve.wait_ge(ms_done, (b + 1) * NT)
                mask_b = maskf[:, b:b + 1, :].to_broadcast([P, NT, M])
                pen_b = pen[:, b:b + 1, :].to_broadcast([P, NT, M])
                src = outp[:, 0:NT * M].rearrange("p (t m) -> p t m", t=NT)
                nc.vector.scalar_tensor_tensor(sc[:, :, :], src, MSCALE, mask_b, ALU.mult, ALU.mult)\
                    .then_inc(ms_masked, 1)
                dve.wait_ge(ms_masked, b + 1)
                link(nc.vector.tensor_tensor(sc[:, :, :], sc[:, :, :], pen_b, ALU.add))
                nc.vector.tensor_reduce(mnegm[:, :], sc[:, :, :], AX.X, ALU.max, negate=True)\
                    .then_inc(ms_max, 1)
                dve.wait_ge(es_ready, (b + 1) * NT)
                link(nc.vector.reciprocal(mrz[:, :], mz[:, :]))
                link(nc.vector.tensor_scalar(mrz[:, :], mrz[:, :], valid[:, b:b + 1], None, ALU.mult))
                bank()
                for t in range(NT):
                    dve.wait_ge(read_done, b * NT + t + 1)
                    nc.vector.scalar_tensor_tensor(x_res[:, b, t], bank()[:, :], mrz[:, t:t + 1],
                                                   x_res[:, b, t], ALU.mult, ALU.add).then_inc(x2_ready, 1)

            def experts(u, b):
                dve.wait_ge(x2_ready, (b + 1) * NT)
                norm(u, b)
                for t in range(NT):
                    dve.wait_ge(xhi_ready, NB * NT + b * NT + t + 1)
                    at = slice(t * P, (t + 1) * P)
                    nc.vector.tensor_tensor(x2T[:, LO, :, at], bank()[:, :].rearrange("p (k n) -> p k n", k=NK),
                                            x2T[:, HI, :, at].bitcast(fp32), ALU.subtract)\
                        .then_inc(xlo_ready, 1)
                for t in range(NT):
                    dve.wait_ge(xa_done, b * NT + t + 1)
                    ins = nc.vector.tensor_tensor(z[:, t, :], sps[t][:, ER:XW], rb1b[:, :], ALU.add)
                    if t < NT - 1:
                        link(ins)
                ins.then_inc(z_ready, 1)
                dve.wait_ge(ez_ready, b + 1)
                link(nc.vector.tensor_scalar(ez[:, :, :], ez[:, :, :], 1.0, None, ALU.add))
                link(nc.vector.reciprocal(ez[:, :, :], ez[:, :, :]))
                nc.vector.tensor_tensor(z[:, :, :], z[:, :, :], ez[:, :, :], ALU.mult).then_inc(h_ready, 1)
                bank()
                dve.wait_ge(lg_done, b + 1)
                nc.vector.tensor_tensor(lg[:, :, :],
                                        bank()[:, 0:NT * NE].rearrange("p (t e) -> p t e", t=NT),
                                        rbgb[:, :].unsqueeze(1).to_broadcast([P, NT, NE]), ALU.add)\
                    .then_inc(lg_ready, 1)
                dve.wait_ge(lg_ready, b + 1)
                for t in range(NT):
                    link(nc.vector.max(out=top[:, t, :], in_=lg[:, t, :]))
                    link(nc.vector.max_index(out=topi[:, t, :], in_max=top[:, t, :], in_values=lg[:, t, :]))
                nc.vector.tensor_tensor(dd[:, :], top[:, :, 1], top[:, :, 0], ALU.subtract)\
                    .then_inc(dd_ready, 1)
                link(nc.vector.tensor_copy(topf[:, :, :], topi[:, :, 0:2]))
                dve.wait_ge(ed_ready, b + 1)
                link(nc.vector.tensor_scalar(dd[:, :], p2[:, :], 1.0, None, ALU.add))
                link(nc.vector.reciprocal(p1[:, :], dd[:, :]))
                link(nc.vector.tensor_tensor(p2[:, :], p2[:, :], p1[:, :], ALU.mult))
                for s, pr in ((0, p1), (1, p2)):
                    link(nc.vector.tensor_tensor(
                        cf[:, s], iot[:, :].unsqueeze(1).to_broadcast([P, NT, NE]),
                        topf[:, :, s:s + 1].to_broadcast([P, NT, NE]), ALU.is_equal))
                    link(nc.vector.tensor_tensor(
                        cf[:, s], cf[:, s], pr[:, :].unsqueeze(2).to_broadcast([P, NT, NE]), ALU.mult))
                link(nc.vector.tensor_tensor(cf[:, 0], cf[:, 0], cf[:, 1], ALU.add))

                def weigh(t):
                    wait(dve, wtr_done, b * NT + t - 1)
                    nc.vector.tensor_tensor(wxa[:, t % 2].rearrange("p (e r) -> p e r", r=RANK),
                                            sps[t][:, 0:ER].rearrange("p (e r) -> p e r", r=RANK),
                                            cf[:, 0, t].unsqueeze(2).to_broadcast([P, NE, RANK]), ALU.mult)\
                        .then_inc(wxa_ready, 1)

                weigh(0)
                for t in range(NT):
                    if t + 1 < NT:
                        weigh(t + 1)
                    dve.wait_ge(wx_hi, b * NT + t + 1)
                    nc.vector.tensor_tensor(wxT[:, t % 2, LO].rearrange("p a n -> p (a n)"), bank()[:, 0:ER],
                                            wxT[:, t % 2, HI].rearrange("p a n -> p (a n)").bitcast(fp32),
                                            ALU.subtract).then_inc(wx_ready, 1)
                    dve.wait_ge(y_mm, b * NT + t + 1)
                    dve.wait_ge(biased, b * NT + t + 1)
                    nc.vector.tensor_tensor(x_res[:, b, t], x_res[:, b, t], colp[:, :], ALU.add)\
                        .then_inc(y_ready, 1)

            dve.wait_ge(prep_done, NK)
            for i, (kind, b) in enumerate(TAIL):
                (memory if kind == "x" else experts)(NB + i, b)


_INS = ["x", "ctx_2048", "mask_BxS2_bk0", "L0_attn_w_qkv", "L0_attn_w_o", "L0_ffn_W", "L0_ffn_bias",
        "L0_ffn_rw1", "L0_ffn_rb1", "L0_ffn_rw2", "L0_ffn_rb2", "L0_ffn_A", "L0_ffn_B", "L0_ffn_gates"]


def kernel(**inputs):
    import numpy as np
    import concourse.bacc as bacc
    from concourse.bass_utils import run_bass_kernel_spmd

    nc = bacc.Bacc("TRN2", target_bir_lowering=False, num_devices=1, dynamic_dma_scratch_size=4096)
    arrays, args = {}, []
    for name in _INS:
        a = np.ascontiguousarray(inputs[name])
        arrays[f"in_{name}"] = a
        args.append(nc.dram_tensor(f"in_{name}", a.shape, mybir.dt.from_np(a.dtype), kind="ExternalInput").ap())
    shape = inputs["x"].shape
    out = nc.dram_tensor("out_0", shape, mybir.dt.float32, kind="ExternalOutput").ap()
    decoder_layer(nc, *args, out)
    r = run_bass_kernel_spmd(nc, [arrays], core_ids=[0])
    return r.results[0]["out_0"]
```

```python
import math
from contextlib import ExitStack

import concourse.bass as bass
from concourse import mybir


def decoder_layer(nc, A_x, A_mem, A_mask, A_wqkv, A_wo, A_W, A_bias, A_rw1, A_rb1, A_rw2, A_rb2,
                  A_A, A_B, A_gates, out):
    fp32 = mybir.dt.float32
    f32r = mybir.dt.float32r
    i32 = mybir.dt.int32
    u32 = mybir.dt.uint32
    ALU = mybir.AluOpType
    ACT = mybir.ActivationFunctionType
    AX = mybir.AxisListType

    P = 128
    NB, SQ, D = A_x.shape
    NT = SQ // P
    NK = D // P
    F = A_wqkv.shape[1] // 3
    DH = P
    NH = F // DH
    NPAIR = NH // 2
    SLOTS = 2 * NB
    NSLOT = NPAIR * SLOTS
    M = A_mem.shape[1]
    NE, RANK = A_A.shape[0], A_A.shape[1]
    ER = NE * RANK
    NA = ER // P
    RH = A_rw1.shape[0]
    XW = ER + RH
    SCALE = 1.0 / math.sqrt(DH)
    MSCALE = 1.0 / math.sqrt(D)
    EPS = 1e-5
    NEG = 1e30
    HI, LO = 0, 1

    x_view = A_x.rearrange("b (t p) d -> p b t d", p=P)
    out_view = out.rearrange("b (t p) d -> p b t d", p=P)
    wqkv_view = A_wqkv.rearrange("(k p) (c n d) -> n c p k d", p=P, c=3, d=DH)
    wo_view = A_wo.rearrange("(q j d) n -> q d j n", j=2, d=DH)

    ctx = ExitStack()
    with ctx:
        def sb(name, shape, dt=fp32):
            return ctx.enter_context(nc.sbuf_tensor(name, shape, dt))

        def sem(name):
            return ctx.enter_context(nc.semaphore(name))

        x_res = sb("x_res", [P, NB, NT, D])
        ident = sb("ident", [P, P])
        big = sb("big", [P, NB, 2 * NK * SQ], f32r)
        xT = big[:, :, :].rearrange("p b (h k n) -> p b h k n", h=2, k=NK)
        wsp = sb("wsp", [P, 2, 2, NK, 3 * DH], f32r)
        wstage = sb("wstage", [P, (NK * 3 * DH + 2 * D)])
        wq_raw = wstage[:, 0:NK * 3 * DH].rearrange("p (k c d) -> p k c d", k=NK, c=3)
        wo_raw = wstage[:, NK * 3 * DH:].rearrange("p (j n) -> p j n", j=2)
        wosp = sb("wosp", [P, 2, 2, D], f32r)
        qk = sb("qk", [P, 2, 2, 2, SQ], f32r)
        work = sb("work", [P, 4, SQ])
        v_sb = work[:, 0:2, :]
        acc = work[:, 2, :]
        val = work[:, 3, :]
        E = sb("E", [P, NT, SQ])
        accsp = sb("accsp", [P, 2, SQ], f32r)
        ones = sb("ones", [P, P], f32r)
        val0 = sb("val0", [P, NB, 2, SQ], f32r)
        val1 = sb("val1", [P, 2, 2, SQ], f32r)
        negm = sb("negm", [P, 2, NT])
        zsum = sb("zsum", [P, 2, NT])
        rz = sb("rz", [P, 2, NT])
        bn = sb("bn", [P, NT, 6])
        mv = sb("mv", [P, NT, 2])
        rstd = sb("rstd", [P, NT])
        m_mv = sb("m_mv", [P, NB * NT, 2])
        m_rstd = sb("m_rstd", [P, NB * NT])
        va = sb("va", [P, NB * NT])
        half = sb("half", [P, NB * NT], i32)
        yt = sb("yt", [P, NB * NT])
        norm_buf = sb("norm_buf", [P, NT, D])
        maskb = sb("maskb", [P, NB, M], A_mask.dtype)
        maskf = sb("maskf", [P, NB, M])
        pen = sb("pen", [P, NB, M])
        valid = sb("valid", [P, NB])
        memT = sb("memT", [P, NB, NK, M])
        sc = sb("sc", [P, NT, M])
        es = sb("es", [P, NT, M])
        mnegm = sb("mnegm", [P, NT])
        mz = sb("mz", [P, NT])
        mrz = sb("mrz", [P, NT])
        biasb = sb("biasb", [P, D])
        rb1b = sb("rb1b", [P, RH])
        rbgb = sb("rbgb", [P, NE])
        gateb = sb("gateb", [P, NE])
        rw2_raw = sb("rw2_raw", [NE, RH])
        rw2T = sb("rw2T", [RH, NE])
        iot = sb("iot", [P, NE])
        z = sb("z", [P, NT, RH])
        ez = sb("ez", [P, NT, RH])
        lg = sb("lg", [P, NT, NE])
        top = sb("top", [P, NT, 8])
        topi = sb("topi", [P, NT, 8], u32)
        topf = sb("topf", [P, NT, 2])
        dd = sb("dd", [P, NT])
        p1 = sb("p1", [P, NT])
        p2 = sb("p2", [P, NT])
        cf = sb("cf", [P, 2, NT, NE])

        WT = big[:, 0].rearrange("p (h k n) -> p h k n", h=2, k=NK)
        XAW = big[:, 1, 0:2 * NK * XW].rearrange("p (h k n) -> p h k n", h=2, k=NK)
        BT = big[:, 2, 0:2 * NA * D].rearrange("p (h a n) -> p h a n", h=2, a=NA)
        wxT = big[:, 2, 2 * NA * D:2 * NA * D + NT * 2 * ER].rearrange("p (s h n) -> p s h n", s=NT, h=2)
        x2T = big[:, 3].rearrange("p (h k n) -> p h k n", h=2, k=NK)
        W_raw = wstage[:, 0:NK * D].rearrange("p (t i) -> p t i", i=D)
        A_raw = wstage[:, 0:NA * D].rearrange("p (a i) -> p a i", i=D)
        B_raw = wstage[:, NA * D:NA * D + NK * ER].rearrange("p (t n) -> p t n", n=ER)
        rw1_raw = wstage[0:RH, NK * D:(NK + 1) * D]
        xa = wstage[:, 0:NT * XW].rearrange("p (t n) -> p t n", t=NT)
        wxa = wstage[:, NT * XW:NT * (XW + ER)].rearrange("p (t n) -> p t n", t=NT)
        x1T = work[:, 0:2, :].rearrange("p s (k n) -> p s k n", k=NK)
        hT = work[0:RH, 2, :]
        eT = work[0:M, 3, :]
        mem_raw = norm_buf[0:M]

        proj = [ctx.enter_context(nc.psum_tensor(f"proj{i}", [P, SQ], fp32)) for i in range(2)]
        sps = [ctx.enter_context(nc.psum_tensor(f"score{i}", [P, SQ], fp32)) for i in range(NT)]
        colp = ctx.enter_context(nc.psum_tensor("colp", [P, SQ], fp32))
        outp = ctx.enter_context(nc.psum_tensor("outp", [P, SQ], fp32))

        x_loaded = [sem(f"x_loaded{b}") for b in range(NB)]
        w_loaded = sem("w_loaded")
        wo_loaded = sem("wo_loaded")
        small_loaded = sem("small_loaded")
        mem_loaded = sem("mem_loaded")
        W_loaded = sem("W_loaded")
        tail_loaded = sem("tail_loaded")
        stored = sem("stored")
        ident_ready = sem("ident_ready")
        ones_ready = sem("ones_ready")
        dve_chain = sem("dve_chain")
        pool_chain = sem("pool_chain")
        xn_ready = sem("xn_ready")
        mn_ready = sem("mn_ready")
        xtr_done = sem("xtr_done")
        xhi_ready = sem("xhi_ready")
        xlo_ready = sem("xlo_ready")
        w_hi = sem("w_hi")
        w_split = sem("w_split")
        wo_hi = sem("wo_hi")
        wo_split = sem("wo_split")
        q_proj = sem("q_proj")
        k_proj = sem("k_proj")
        v_proj = sem("v_proj")
        q_hi = sem("q_hi")
        k_hi = sem("k_hi")
        q_split = sem("q_split")
        k_split = sem("k_split")
        v_copied = sem("v_copied")
        s_done = sem("s_done")
        max_ready = sem("max_ready")
        e_ready = sem("e_ready")
        rz_ready = sem("rz_ready")
        acc_step = sem("acc_step")
        acc_hi = sem("acc_hi")
        acc_split = sem("acc_split")
        c_done = sem("c_done")
        val_ready = sem("val_ready")
        val_hi = sem("val_hi")
        val_split = sem("val_split")
        o_done = sem("o_done")
        o_added = sem("o_added")
        prep_done = sem("prep_done")
        prep_hi = sem("prep_hi")
        prep_ready = sem("prep_ready")
        memtr_done = sem("memtr_done")
        memT_ready = sem("memT_ready")
        m_norms = sem("m_norms")
        x1_ready = sem("x1_ready")
        ms_done = sem("ms_done")
        ms_masked = sem("ms_masked")
        ms_max = sem("ms_max")
        es_ready = sem("es_ready")
        etr_done = sem("etr_done")
        eT_ready = sem("eT_ready")
        read_done = sem("read_done")
        x2_ready = sem("x2_ready")
        xa_done = sem("xa_done")
        xa_copied = sem("xa_copied")
        z_ready = sem("z_ready")
        ez_ready = sem("ez_ready")
        h_ready = sem("h_ready")
        htr_done = sem("htr_done")
        hT_ready = sem("hT_ready")
        lg_done = sem("lg_done")
        lg_ready = sem("lg_ready")
        cf_ready = sem("cf_ready")
        dd_ready = sem("dd_ready")
        ed_ready = sem("ed_ready")
        wxa_ready = sem("wxa_ready")
        wtr_done = sem("wtr_done")
        wx_hi = sem("wx_hi")
        wx_full = sem("wx_full")
        wx_ready = sem("wx_ready")
        biased = sem("biased")
        y_mm = sem("y_mm")
        y_ready = sem("y_ready")

        def wait(eng, semaphore, value):
            if not isinstance(value, int) or value > 0:
                eng.wait_ge(semaphore, value)

        def is_first(p):
            return isinstance(p, int) and p == 0

        NPREP = NK + NK + NA

        def is_last(p):
            return isinstance(p, int) and p == NPAIR - 1

        def pairs(eng, body):
            body(0)
            with eng.Fori(1, NPAIR - 1) as p:
                body(p)
            body(NPAIR - 1)

        NORMS = [("a", b) for b in range(NB)] + [("m", 0), ("m", 1)]
        for b in range(NB):
            NORMS += [("x", b)] + [("m", b + 2)] * (b + 2 < NB)
        number = {what: u for u, what in enumerate(NORMS)}
        TURNS = [("xaw", k) for k in range(NK)] + [("m", 0, t) for t in range(NT)]
        TURNS += [("bt", a) for a in range(NA)] + [("rw2",), ("e", 0)] + [("r", 0, t) for t in range(NT)]
        PRODUCTS = [("ms", 0)]
        for b in range(NB):
            more = b + 1 < NB
            TURNS += [("m", b + 1, t) for t in range(NT * more)] + [("x", b, t) for t in range(NT)]
            TURNS += [("h", b), ("l", b)] + [("e", b + 1)] * more + [("r", b + 1, t) for t in range(NT * more)]
            TURNS += [("w", b, t) for t in range(NT)]
            PRODUCTS += [("ms", b + 1)] * more + [("xa", b, t) for t in range(NT)]

        def turn_bank(*what):
            return proj[TURNS.index(what) % 2]

        def product_bank(*what):
            return (colp, outp)[PRODUCTS.index(what) % 2]

        def first_bank(b, t):
            return sps[t] if b == 0 else outp if t % 2 == 0 else proj[b % 2]

        block = ctx.enter_context(nc.Block())

        @block.sync
        def _(sp):
            def load_w(h):
                for c in range(3):
                    sp.dma_start(wq_raw[:, :, c, :], wqkv_view[h, c]).then_inc(w_loaded, 16)

            sp.dma_start(x_res[:, 0], x_view[:, 0]).then_inc(x_loaded[0], 16)
            load_w(0)
            for b in range(1, NB):
                sp.dma_start(x_res[:, b], x_view[:, b]).then_inc(x_loaded[b], 16)

            def pair(p):
                sp.wait_ge(w_split, p * 2 + 1)
                load_w(p * 2 + 1)
                wait(sp, wo_split, p)
                sp.dma_start(wo_raw, wo_view[p]).then_inc(wo_loaded, 16)
                if is_first(p):
                    sp.dma_start(maskb[:, :, :], A_mask.partition_broadcast(P)).then_inc(small_loaded, 16)
                    sp.dma_start(biasb[:, :], A_bias.partition_broadcast(P)).then_inc(small_loaded, 16)
                    sp.dma_start(rb1b[:, :], A_rb1.partition_broadcast(P)).then_inc(small_loaded, 16)
                    sp.dma_start(rbgb[:, :], A_rb2[0:NE].partition_broadcast(P)).then_inc(small_loaded, 16)
                    sp.dma_start(gateb[:, :], A_gates.partition_broadcast(P)).then_inc(small_loaded, 16)
                    sp.dma_start(rw2_raw[:, :], A_rw2[0:NE, :]).then_inc(small_loaded, 16)
                if not is_last(p):
                    sp.wait_ge(w_split, p * 2 + 2)
                    load_w(p * 2 + 2)
                if is_first(p):
                    sp.wait_ge(xtr_done, NB * NT)
                    sp.dma_start(mem_raw, A_mem.rearrange("b m d -> m b d")).then_inc(mem_loaded, 16)

            pairs(sp, pair)
            sp.wait_ge(w_split, NH)
            sp.wait_ge(wo_split, NPAIR)
            sp.dma_start(W_raw, A_W.rearrange("(t p) i -> p t i", p=P)).then_inc(W_loaded, 16)
            sp.dma_start(rw1_raw, A_rw1).then_inc(tail_loaded, 16)
            sp.wait_ge(prep_done, NK)
            sp.dma_start(A_raw, A_A.rearrange("e r i -> (e r) i").rearrange("(a p) i -> p a i", p=P))\
                .then_inc(tail_loaded, 16)
            b_view = A_B.rearrange("e (t p) r -> t p e r", p=P)
            for t in range(D // P):
                sp.dma_start(B_raw[:, t, :].rearrange("p (e r) -> p e r", r=RANK), b_view[t])\
                    .then_inc(tail_loaded, 16)
            for b in range(NB - 1):
                sp.wait_ge(y_ready, NT * (b + 1))
                sp.dma_start(out_view[:, b], x_res[:, b]).then_inc(stored, 16)
            for t in range(NT):
                sp.wait_ge(y_ready, NT * (NB - 1) + t + 1)
                sp.dma_start(out_view[:, NB - 1, t], x_res[:, NB - 1, t]).then_inc(stored, 16)
            sp.wait_ge(stored, 16 * (NB - 1 + NT))

        @block.gpsimd
        def _(pool):
            chain = [0]

            def link(ins):
                chain[0] += 1
                ins.then_inc(pool_chain, 1)
                pool.wait_ge(pool_chain, chain[0])

            link(nc.gpsimd.memset(ident[:, :], 0.0))
            nc.gpsimd.affine_select(out=ident[:, :], in_=ident[:, :], compare_op=ALU.not_equal, fill=1.0,
                                    base=0, pattern=[[-1, P]], channel_multiplier=1).then_inc(ident_ready, 1)
            nc.gpsimd.memset(ones[:, :].bitcast(fp32), 1.0).then_inc(ones_ready, 1)
            pool.wait_ge(ones_ready, 1)
            link(nc.gpsimd.iota(iot[:, :], pattern=[[1, NE]], base=0, channel_multiplier=0,
                                allow_small_or_imprecise_dtypes=True))

            def high(dst, src):
                one = ones[:, 0:1].bitcast(fp32).to_broadcast([P, src.shape[1]])
                return nc.gpsimd.tensor_tensor(dst, src, one, ALU.mult)

            def split_w(h, parity):
                pool.wait_ge(w_loaded, h * 48 + 48)
                raw = wstage[:, 0:NK * 3 * DH]
                hi, lo = (wsp[:, parity, f].rearrange("p k n -> p (k n)") for f in (HI, LO))
                high(hi, raw).then_inc(w_hi, 1)
                pool.wait_ge(w_hi, h + 1)
                nc.gpsimd.tensor_tensor(lo, raw, hi.bitcast(fp32), ALU.subtract).then_inc(w_split, 1)

            def slot(p, j):
                n1 = p * SLOTS + j
                if not (is_first(p) and j == 0):
                    b, head = (j - 1) % NB, (j - 1) // NB % 2
                    pool.wait_ge(acc_step, n1 * NT)
                    wait(pool, c_done, n1 - 1)
                    high(accsp[:, HI], acc).then_inc(acc_hi, 1)
                    pool.wait_ge(acc_hi, n1)
                    nc.gpsimd.tensor_tensor(accsp[:, LO], acc, accsp[:, HI].bitcast(fp32),
                                            ALU.subtract).then_inc(acc_split, 1)
                    pool.wait_ge(val_ready, n1)
                    if head == 0 or j == 0:
                        dst = val0[:, b] if head == 0 else val1[:, b % 2]
                    else:
                        dst = val1[:, b % 2]
                    if head == 0:
                        wait(pool, o_done, p * (NB * NT) + (b + 1 - NB) * NT)
                    elif j == 0:
                        wait(pool, o_done, p * (NB * NT) + (b - 1 - NB) * NT)
                    else:
                        wait(pool, o_done, p * (NB * NT) + (b - 1) * NT)
                    high(dst[:, HI], val).then_inc(val_hi, 1)
                    pool.wait_ge(val_hi, n1)
                    nc.gpsimd.tensor_tensor(dst[:, LO], val, dst[:, HI].bitcast(fp32),
                                            ALU.subtract).then_inc(val_split, 1)
                if j == 1 or (j == 1 + NB and not is_last(p)):
                    h = p * 2 + (1 if j == 1 else 2)
                    wait(pool, v_proj, h * NB - NB)
                    split_w(h, 1 if j == 1 else 0)
                if j == 3:
                    pool.wait_ge(wo_loaded, p * 16 + 16)
                    wait(pool, o_done, p * (NB * NT))
                    raw = wstage[:, NK * 3 * DH:]
                    hi, lo = (wosp[:, f].rearrange("p j n -> p (j n)") for f in (HI, LO))
                    high(hi, raw).then_inc(wo_hi, 1)
                    pool.wait_ge(wo_hi, p + 1)
                    nc.gpsimd.tensor_tensor(lo, raw, hi.bitcast(fp32), ALU.subtract).then_inc(wo_split, 1)

            def pair(p):
                for j in range(SLOTS):
                    slot(p, j)

            split_w(0, 0)
            pairs(pool, pair)
            slot(NPAIR, 0)

            def apply_norm(b):
                u = number["m", b]
                pool.wait_ge(m_norms, 1 if b == 0 else 2)
                for t in range(NT):
                    if b == 0:
                        pool.wait_ge(acc_step, NSLOT * NT)
                    else:
                        pool.wait_ge(xtr_done, (u - 1) * NT + t + 1)
                    i = b * NT + t
                    nc.gpsimd.tensor_scalar(E[:, t, :], x_res[:, b, t], m_mv[:, i, 0:1], m_rstd[:, i:i + 1],
                                            ALU.subtract, ALU.mult).then_inc(mn_ready, 1)

            apply_norm(0)
            apply_norm(1)
            for b in range(NB):
                pool.wait_ge(xn_ready, NT * (NB + b + 1))
                for t in range(NT):
                    nc.gpsimd.tensor_tensor(x_res[:, b, t], x_res[:, b, t], biasb[:, :], ALU.add)\
                        .then_inc(biased, 1)
                if b + 2 < NB:
                    apply_norm(b + 2)
                pool.wait_ge(cf_ready, b + 1)
                for t in range(NT):
                    nc.gpsimd.tensor_tensor(wxa[:, t].rearrange("p (e r) -> p e r", r=RANK),
                                            xa[:, t, 0:ER].rearrange("p (e r) -> p e r", r=RANK),
                                            cf[:, 0, t].unsqueeze(2).to_broadcast([P, NE, RANK]), ALU.mult)\
                        .then_inc(wxa_ready, 1)
                for t in range(NT):
                    pool.wait_ge(wx_full, b * NT + t + 1)
                    nc.gpsimd.tensor_tensor(wxT[:, t, LO], wxa[:, t], wxT[:, t, HI].bitcast(fp32),
                                            ALU.subtract).then_inc(wx_ready, 1)

        @block.tensor
        def _(pe):
            def halves(out_ap, lhsT, rhs, start, stop):
                nc.tensor.matmul(out_ap, lhsT(HI), rhs(HI), start=start, stop=False)
                nc.tensor.matmul(out_ap, lhsT(HI), rhs(LO), start=False, stop=False)
                return nc.tensor.matmul(out_ap, lhsT(LO), rhs(HI), start=False, stop=stop)

            def turn_tile(bank, src):
                for k in range(NK):
                    mm = nc.tensor.transpose(bank[:, k * P:(k + 1) * P], src[:, k * P:(k + 1) * P], ident[:, :])
                return mm

            def first_turn(b, t):
                pe.wait_ge(xn_ready, b * NT + t + 1)
                if b > 0 and t > 1:
                    pe.wait_ge(xlo_ready, b * NT + t - 1)
                elif b > 1:
                    pe.wait_ge(xlo_ready, (b - 1) * NT + t + 3)
                if b > 1 and t == 1:
                    pe.wait_ge(v_copied, b - 1)
                turn_tile(first_bank(b, t), norm_buf[:, t, :]).then_inc(xtr_done, 1)

            def project(c, b, parity, bank):
                for k in range(NK):
                    mm = halves(proj[bank][:, :],
                                lambda f: wsp[:, parity, f, k, c * DH:(c + 1) * DH],
                                lambda f: xT[:, b, f, k, :], k == 0, k == NK - 1)
                return mm

            def q_project(p, j, n):
                b, head = j % NB, j // NB % 2
                if b == 0:
                    pe.wait_ge(w_split, p * 2 + (j // NB) + 1)
                if is_first(p) and 0 < j < NB:
                    pe.wait_ge(xlo_ready, (j + 1) * NT)
                    pe.wait_ge(v_copied, n)
                else:
                    wait(pe, k_split, n)
                project(0, b, head, (n_parity(j - 1) * 3) % 2).then_inc(q_proj, 1)

            def n_parity(j):
                return j % 2

            def k_project(p, j, n):
                wait(pe, v_copied, n - 1)
                project(1, j % NB, j // NB % 2, (n_parity(j - 1) * 3 + 1) % 2).then_inc(k_proj, 1)

            def v_project(p, j, n, has_next):
                if is_first(p) and j < NB - 1:
                    pe.wait_ge(k_split, n + 1)
                elif has_next:
                    pe.wait_ge(q_split, n + 2)
                project(2, j % NB, j // NB % 2, (n_parity(j) * 3 + 2) % 2).then_inc(v_proj, 1)

            def scores(j, n, t):
                if t == 0:
                    pe.wait_ge(q_split, n + 1)
                    pe.wait_ge(k_split, n + 1)
                wait(pe, e_ready, n * NT + (t + 1 - NT))
                halves(sps[t][:, :], lambda f: qk[:, j % 2, 0, f, t * P:(t + 1) * P],
                       lambda f: qk[:, j % 2, 1, f, :], True, True).then_inc(s_done, 1)

            def column_sums(n):
                pe.wait_ge(acc_split, n)
                wait(pe, val_ready, n - 1)
                nc.tensor.matmul(colp[:, :], ones[:, :], accsp[:, HI], start=True, stop=False)
                nc.tensor.matmul(colp[:, :], ones[:, :], accsp[:, LO], start=False, stop=True)\
                    .then_inc(c_done, 1)

            def out_tile(p, b, t):
                if t == 0:
                    pe.wait_ge(val_split, p * SLOTS + NB + b + 1)
                    if b == 0:
                        pe.wait_ge(wo_split, p + 1)
                wait(pe, o_added, p * (NB * NT) + b * NT + t)
                if is_last(p) and b == 0 and t == 0:
                    pe.wait_ge(prep_ready, NK)
                halves(outp[:, :], lambda f: val0[:, b, f, t * P:(t + 1) * P],
                       lambda f: wosp[:, f, 0, :], True, False)
                halves(outp[:, :], lambda f: val1[:, b % 2, f, t * P:(t + 1) * P],
                       lambda f: wosp[:, f, 1, :], False, True).then_inc(o_done, 1)

            def slot(p, j):
                n = p * SLOTS + j
                has_next = not (is_last(p) and j == SLOTS - 1)
                outs = []
                if j >= NB + 2:
                    outs = [(p, j - 2 - NB, t) for t in range(NT)]
                elif j < 2 and not is_first(p):
                    outs = [(p - 1, j + NB - 2, t) for t in range(NT)]

                def some(k):
                    if outs:
                        out_tile(*outs[k])

                    if is_last(p) and j == NB:
                        turn_memory(k)
                    if is_last(p) and j == NB + 1:
                        turn_W(k)

                if is_first(p) and j < NB - 1:
                    scores(j, n, 0)
                    scores(j, n, 1)
                    v_project(p, j, n, True)
                    scores(j, n, 2)
                    scores(j, n, 3)
                    for t in range(NT):
                        first_turn(j + 1, t)
                    q_project(p, j + 1, n + 1)
                    if j > 0:
                        column_sums(n)
                    k_project(p, j + 1, n + 1)
                    return
                if has_next:
                    q_project(p, j + 1, n + 1)
                some(0)
                scores(j, n, 0)
                scores(j, n, 1)
                some(1)
                if has_next:
                    k_project(p, j + 1, n + 1)
                if not (is_first(p) and j == 0):
                    column_sums(n)
                some(2)
                scores(j, n, 2)
                scores(j, n, 3)
                v_project(p, j, n, has_next)
                some(3)

            def turn_memory(b):
                if b == 0:
                    pe.wait_ge(mem_loaded, 16)
                    pe.wait_ge(o_added, (NPAIR - 1) * NB * NT)
                else:
                    pe.wait_ge(memT_ready, b)
                for k in range(NK):
                    mm = nc.tensor.matmul(outp[:, k * M:(k + 1) * M], mem_raw[:, b, k * P:(k + 1) * P],
                                          ident[0:M, 0:M], start=True, stop=True)
                mm.then_inc(memtr_done, 1)

            def turn_W(k):
                if k == 0:
                    pe.wait_ge(W_loaded, 16)
                    pe.wait_ge(memT_ready, NB)
                else:
                    pe.wait_ge(prep_ready, k)
                for t in range(D // P):
                    mm = nc.tensor.transpose(outp[:, t * P:(t + 1) * P], W_raw[:, t, k * P:(k + 1) * P],
                                             ident[:, :])
                mm.then_inc(prep_done, 1)

            def pair(p):
                for j in range(SLOTS):
                    slot(p, j)

            pe.wait_ge(ident_ready, 1)
            for t in range(NT):
                first_turn(0, t)
            pe.wait_ge(ones_ready, 1)
            pe.wait_ge(xlo_ready, NT)
            q_project(0, 0, 0)
            k_project(0, 0, 0)
            pairs(pe, pair)

            def released(what):
                kind, b, t = (*what, 0, 0)[:3]
                return {"xaw": (prep_ready, NK + b + 1), "bt": (prep_ready, 2 * NK + b + 1),
                        "rw2": (prep_ready, NPREP + 1), "m": (x1_ready, b * NT + t + 1),
                        "x": (xlo_ready, (NB + b) * NT + t + 1), "h": (hT_ready, b + 1),
                        "l": (lg_ready, b + 1), "e": (eT_ready, b + 1), "r": (x2_ready, b * NT + t + 1),
                        "w": (wx_full, b * NT + t + 1), "ms": (ms_masked, b + 1),
                        "xa": (xa_copied, b * NT + t + 1)}[kind]

            def take_turn(*what):
                i = TURNS.index(what)
                pe.wait_ge(*(released(TURNS[i - 2]) if i >= 2 else (v_copied, NSLOT - 1 + i)))
                return turn_bank(*what)

            def take_product(*what):
                i = PRODUCTS.index(what)
                if i >= 2:
                    pe.wait_ge(*released(PRODUCTS[i - 2]))
                elif i == 0:
                    pe.wait_ge(val_ready, NSLOT)
                else:
                    pe.wait_ge(o_added, NPAIR * NB * NT)
                return product_bank(*what)

            def turned(kind, b, t):
                if kind == "m":
                    pe.wait_ge(mn_ready, b * NT + t + 1)
                else:
                    pe.wait_ge(xn_ready, (NB + b) * NT + t + 1)
                turn_tile(take_turn(kind, b, t), E[:, t, :]).then_inc(xtr_done, 1)

            def turn_xaw(k):
                bank = take_turn("xaw", k)
                for a in range(NA):
                    nc.tensor.transpose(bank[:, a * P:(a + 1) * P], A_raw[:, a, k * P:(k + 1) * P], ident[:, :])
                nc.tensor.matmul(bank[:, ER:XW], rw1_raw[:, k * P:(k + 1) * P], ident[0:RH, 0:RH],
                                 start=True, stop=True).then_inc(prep_done, 1)

            def turn_bt(a):
                bank = take_turn("bt", a)
                for t in range(D // P):
                    mm = nc.tensor.transpose(bank[:, t * P:(t + 1) * P], B_raw[:, t, a * P:(a + 1) * P],
                                             ident[:, :])
                mm.then_inc(prep_done, 1)

            def memory_scores(b):
                bank = None
                for t in range(NT + 1):
                    if t < NT:
                        turned("m", b, t)
                    if t >= 1:
                        if t == 1:
                            bank = take_product("ms", b)
                        pe.wait_ge(x1_ready, b * NT + t)
                        for k in range(NK):
                            mm = nc.tensor.matmul(bank[:, (t - 1) * M:t * M], x1T[:, (t - 1) % 2, k, :],
                                                  memT[:, b, k, :], start=(k == 0), stop=(k == NK - 1))
                        mm.then_inc(ms_done, 1)

            def turn_probabilities(b):
                pe.wait_ge(es_ready, (b + 1) * NT)
                bank = take_turn("e", b)
                for t in range(NT):
                    mm = nc.tensor.matmul(bank[0:M, t * P:(t + 1) * P], es[:, t, :], ident[:, :],
                                          start=True, stop=True)
                mm.then_inc(etr_done, 1)

            def readout(b):
                pe.wait_ge(eT_ready, b + 1)
                for t in range(NT):
                    nc.tensor.matmul(take_turn("r", b, t)[:, :], eT[:, t * P:(t + 1) * P], mem_raw[:, b, :],
                                     start=True, stop=True).then_inc(read_done, 1)

            def first_product(b):
                for t in range(NT + 1):
                    if t < NT:
                        turned("x", b, t)
                    if t >= 1:
                        pe.wait_ge(xlo_ready, (NB + b) * NT + t)
                        bank = take_product("xa", b, t - 1)
                        for k in range(NK):
                            mm = halves(bank[:, 0:XW], lambda f: x2T[:, f, k, (t - 1) * P:t * P],
                                        lambda f: XAW[:, f, k, :], k == 0, k == NK - 1)
                        mm.then_inc(xa_done, 1)

            def turn_h(b):
                pe.wait_ge(h_ready, b + 1)
                bank = take_turn("h", b)
                for t in range(NT):
                    mm = nc.tensor.matmul(bank[0:RH, t * P:(t + 1) * P], z[:, t, :], ident[:, :],
                                          start=True, stop=True)
                mm.then_inc(htr_done, 1)

            def logits(b):
                pe.wait_ge(hT_ready, b + 1)
                bank = take_turn("l", b)
                for t in range(NT):
                    mm = nc.tensor.matmul(bank[:, t * NE:(t + 1) * NE], hT[:, t * P:(t + 1) * P],
                                          rw2T[:, :], start=True, stop=True)
                mm.then_inc(lg_done, 1)

            def base(b, t):
                wait(pe, y_ready, (b - 1) * NT + t + 1)
                for k in range(NK):
                    halves(sps[t][:, :], lambda f: x2T[:, f, k, t * P:(t + 1) * P],
                           lambda f: WT[:, f, k, :], k == 0, False)

            def turn_weighed(b, t):
                pe.wait_ge(wxa_ready, b * NT + t + 1)
                bank = take_turn("w", b, t)
                for a in range(NA):
                    mm = nc.tensor.transpose(bank[:, a * P:(a + 1) * P], wxa[:, t, a * P:(a + 1) * P],
                                             ident[:, :])
                mm.then_inc(wtr_done, 1)

            def delta(b, t):
                pe.wait_ge(wx_ready, b * NT + t + 1)
                for a in range(NA):
                    mm = halves(sps[t][:, :], lambda f: wxT[:, t, f, a * P:(a + 1) * P],
                                lambda f: BT[:, f, a, :], False, a == NA - 1)
                mm.then_inc(y_mm, 1)

            last = NPAIR - 1
            out_tile(last, NB - 2, 0)
            out_tile(last, NB - 2, 1)
            column_sums(NSLOT)
            out_tile(last, NB - 2, 2)
            out_tile(last, NB - 2, 3)
            pe.wait_ge(tail_loaded, 16 * (2 + D // P))
            for k in range(NK):
                turn_xaw(k)
            for t in range(NT):
                out_tile(last, NB - 1, t)
            memory_scores(0)
            for a in range(NA):
                turn_bt(a)
            pe.wait_ge(small_loaded, 16 * 6)
            nc.tensor.matmul(take_turn("rw2")[0:RH, 0:NE], rw2_raw[:, :], ident[0:NE, 0:NE],
                             start=True, stop=True).then_inc(prep_done, 1)
            turn_probabilities(0)
            readout(0)
            pe.wait_ge(prep_ready, NPREP + 1)
            for b in range(NB):
                more = b + 1 < NB
                if more:
                    memory_scores(b + 1)
                first_product(b)
                base(b, 0)
                turn_h(b)
                base(b, 1)
                logits(b)
                base(b, 2)
                if more:
                    turn_probabilities(b + 1)
                    readout(b + 1)
                for t in range(NT):
                    turn_weighed(b, t)
                base(b, 3)
                for t in range(NT):
                    delta(b, t)

        @block.scalar
        def _(act):
            def first_high(b, t):
                act.wait_ge(xtr_done, b * NT + t + 1)
                nc.scalar.activation(xT[:, b, HI, :, t * P:(t + 1) * P],
                                     first_bank(b, t)[:, :].rearrange("p (k n) -> p k n", k=NK), ACT.Copy)\
                    .then_inc(xhi_ready, 1)

            def q_high(j, n):
                act.wait_ge(q_proj, n + 1)
                wait(act, s_done, n * NT - NT)
                nc.scalar.activation(qk[:, j % 2, 0, HI], proj[((j - 1) % 2 * 3) % 2][:, :], ACT.Copy,
                                     scale=SCALE).then_inc(q_hi, 1)

            def k_high(j, n):
                act.wait_ge(k_proj, n + 1)
                nc.scalar.activation(qk[:, j % 2, 1, HI], proj[((j - 1) % 2 * 3 + 1) % 2][:, :], ACT.Copy)\
                    .then_inc(k_hi, 1)

            def exponentials(j, n, t):
                act.wait_ge(max_ready, n * NT + t + 1)
                wait(act, acc_step, n * NT + (t + 1 - NT))
                nc.scalar.activation(E[:, t, :], sps[t][:, :], ACT.Exp, bias=negm[:, j % 2, t:t + 1],
                                     accum_out=zsum[:, j % 2, t:t + 1]).then_inc(e_ready, 1)

            def slot(p, j):
                n = p * SLOTS + j
                has_next = not (is_last(p) and j == SLOTS - 1)
                early = is_first(p) and j < NB - 1
                if has_next and not early:
                    q_high(j + 1, n + 1)
                prepare(p, j, 0)
                exponentials(j, n, 0)
                exponentials(j, n, 1)
                prepare(p, j, 1)
                if early:
                    copy_values(j, n)
                elif has_next:
                    k_high(j + 1, n + 1)
                prepare(p, j, 2)
                exponentials(j, n, 2)
                exponentials(j, n, 3)
                if early:
                    for t in range(NT):
                        first_high(j + 1, t)
                    q_high(j + 1, n + 1)
                    k_high(j + 1, n + 1)
                else:
                    copy_values(j, n)
                prepare(p, j, 3)

            def copy_values(j, n):
                act.wait_ge(v_proj, n + 1)
                wait(act, val_ready, n - 1)
                nc.scalar.activation(v_sb[:, j % 2], proj[(j % 2 * 3 + 2) % 2][:, :], ACT.Copy)\
                    .then_inc(v_copied, 1)

            def prepare(p, j, k):
                if is_last(p) and j == NB:
                    act.wait_ge(memtr_done, k + 1)
                    nc.scalar.activation(memT[:, k].rearrange("p k m -> p (k m)"), outp[:, 0:NK * M],
                                         ACT.Copy).then_inc(memT_ready, 1)
                if is_last(p) and j == NB + 1:
                    act.wait_ge(prep_done, k + 1)
                    act.wait_ge(v_proj, NSLOT - NB + 1)
                    nc.scalar.activation(WT[:, HI, k], outp[:, :], ACT.Copy).then_inc(prep_hi, 1)

            def pair(p):
                for j in range(SLOTS):
                    slot(p, j)

            for t in range(NT):
                first_high(0, t)
            q_high(0, 0)
            k_high(0, 0)
            pairs(act, pair)

            def memory_tiles(b):
                for t in range(NT):
                    act.wait_ge(xtr_done, number["m", b] * NT + t + 1)
                    wait(act, ms_done, b * NT + t - 1)
                    if b == 0 and t < 2:
                        act.wait_ge(val_ready, NSLOT)
                    nc.scalar.activation(x1T[:, t % 2], turn_bank("m", b, t)[:, :].rearrange(
                        "p (k n) -> p k n", k=NK), ACT.Copy).then_inc(x1_ready, 1)

            def memory_exponentials(b):
                act.wait_ge(ms_max, b + 1)
                for t in range(NT):
                    nc.scalar.activation(es[:, t, :], sc[:, t, :], ACT.Exp, bias=mnegm[:, t:t + 1],
                                         accum_out=mz[:, t:t + 1]).then_inc(es_ready, 1)

            def memory_turned(b):
                act.wait_ge(etr_done, b + 1)
                if b == 0:
                    act.wait_ge(val_split, NSLOT)
                nc.scalar.activation(eT, turn_bank("e", b)[0:M, :], ACT.Copy).then_inc(eT_ready, 1)

            def high(b, t):
                act.wait_ge(xtr_done, number["x", b] * NT + t + 1)
                wait(act, y_mm, (b - 1) * NT + t + 1)
                nc.scalar.activation(x2T[:, HI, :, t * P:(t + 1) * P], turn_bank("x", b, t)[:, :].rearrange(
                    "p (k n) -> p k n", k=NK), ACT.Copy).then_inc(xhi_ready, 1)

            def copy_xa(b, t):
                act.wait_ge(xa_done, b * NT + t + 1)
                wait(act, wxa_ready, (b - 1) * NT + t + 1)
                nc.scalar.activation(xa[:, t, :], product_bank("xa", b, t)[:, 0:XW], ACT.Copy)\
                    .then_inc(xa_copied, 1)

            for k in range(NK):
                act.wait_ge(prep_done, NK + k + 1)
                nc.scalar.activation(XAW[:, HI, k], turn_bank("xaw", k)[:, 0:XW], ACT.Copy).then_inc(prep_hi, 1)
            memory_tiles(0)
            memory_exponentials(0)
            for a in range(NA):
                act.wait_ge(prep_done, 2 * NK + a + 1)
                nc.scalar.activation(BT[:, HI, a], turn_bank("bt", a)[:, :], ACT.Copy).then_inc(prep_hi, 1)
            memory_turned(0)
            for b in range(NB):
                more = b + 1 < NB
                if more:
                    memory_tiles(b + 1)
                high(b, 0)
                high(b, 1)
                if more:
                    memory_exponentials(b + 1)
                copy_xa(b, 0)
                high(b, 2)
                copy_xa(b, 1)
                high(b, 3)
                copy_xa(b, 2)
                copy_xa(b, 3)
                act.wait_ge(z_ready, b + 1)
                nc.scalar.activation(ez[:, :, :], z[:, :, :], ACT.Exp, scale=-1.0).then_inc(ez_ready, 1)
                act.wait_ge(htr_done, b + 1)
                nc.scalar.activation(hT, turn_bank("h", b)[0:RH, :], ACT.Copy).then_inc(hT_ready, 1)
                act.wait_ge(dd_ready, b + 1)
                nc.scalar.activation(p2[:, :], dd[:, :], ACT.Exp).then_inc(ed_ready, 1)
                if more:
                    memory_turned(b + 1)
                for t in range(NT):
                    act.wait_ge(wtr_done, b * NT + t + 1)
                    wait(act, y_mm, (b - 1) * NT + t + 1)
                    nc.scalar.activation(wxT[:, t, HI], turn_bank("w", b, t)[:, 0:ER], ACT.Copy)\
                        .then_inc(wx_hi, 1)
                    nc.scalar.activation(wxa[:, t], turn_bank("w", b, t)[:, 0:ER], ACT.Copy)\
                        .then_inc(wx_full, 1)

        @block.vector
        def _(dve):
            chain = [0]

            def link(ins):
                chain[0] += 1
                ins.then_inc(dve_chain, 1)
                dve.wait_ge(dve_chain, chain[0])

            def statistics(b, t, out_mv):
                link(nc.vector.bn_stats(bn[:, t], x_res[:, b, t]))
                nc.vector.bn_aggr(out_mv, bn[:, t]).then_inc(dve_chain, 1)
                chain[0] += 1

            def inverse_deviation(y, variance, n):
                v, h, w = va[:, 0:n], half[:, 0:n], yt[:, 0:n]
                dve.wait_ge(dve_chain, chain[0])
                link(nc.vector.tensor_scalar(v, variance, EPS, None, ALU.add))
                link(nc.vector.tensor_scalar(h, v.bitcast(i32), 1, None, ALU.logical_shift_right))
                link(nc.vector.tensor_scalar(y.bitcast(i32), h, -1.0, float(0x5F3759DF), ALU.mult, ALU.add))
                for step in range(3):
                    link(nc.vector.tensor_tensor(w, y, y, ALU.mult))
                    link(nc.vector.scalar_tensor_tensor(w, w, -0.5, v, ALU.mult, ALU.mult))
                    last = nc.vector.scalar_tensor_tensor(y, w, 1.5, y, ALU.add, ALU.mult)
                    if step < 2:
                        link(last)
                return last

            def apply_norm(u, b, dst):
                for t in range(NT):
                    wait(dve, xtr_done, (u - 1) * NT + t + 1)
                    nc.vector.tensor_scalar(dst[:, t, :], x_res[:, b, t], mv[:, t, 0:1], rstd[:, t:t + 1],
                                            ALU.subtract, ALU.mult).then_inc(xn_ready, 1)

            def first_statistics(b):
                dve.wait_ge(x_loaded[b], 16)
                for t in range(NT):
                    statistics(b, t, mv[:, t])

            def first_low(b):
                for t in range(NT):
                    dve.wait_ge(xhi_ready, b * NT + t + 1)
                    at = slice(t * P, (t + 1) * P)
                    nc.vector.tensor_tensor(xT[:, b, LO, :, at],
                                            first_bank(b, t)[:, :].rearrange("p (k n) -> p k n", k=NK),
                                            xT[:, b, HI, :, at].bitcast(fp32), ALU.subtract)\
                        .then_inc(xlo_ready, 1)

            def q_low(j, n):
                dve.wait_ge(q_hi, n + 1)
                nc.vector.scalar_tensor_tensor(qk[:, j % 2, 0, LO], proj[((j - 1) % 2 * 3) % 2][:, :], SCALE,
                                               qk[:, j % 2, 0, HI].bitcast(fp32), ALU.mult, ALU.subtract)\
                    .then_inc(q_split, 1)

            def k_low(j, n):
                dve.wait_ge(k_hi, n + 1)
                nc.vector.tensor_tensor(qk[:, j % 2, 1, LO], proj[((j - 1) % 2 * 3 + 1) % 2][:, :],
                                        qk[:, j % 2, 1, HI].bitcast(fp32), ALU.subtract)\
                    .then_inc(k_split, 1)

            def maximum(j, n, t):
                dve.wait_ge(s_done, n * NT + t + 1)
                nc.vector.tensor_reduce(negm[:, j % 2, t:t + 1], sps[t][:, :], AX.X, ALU.max, negate=True)\
                    .then_inc(max_ready, 1)

            def add_out(p, b, t):
                dve.wait_ge(o_done, p * (NB * NT) + b * NT + t + 1)
                nc.vector.tensor_tensor(x_res[:, b, t], x_res[:, b, t], outp[:, :], ALU.add)\
                    .then_inc(o_added, 1)

            def values(j, n):
                dve.wait_ge(c_done, n)
                dve.wait_ge(v_copied, n)
                wait(dve, val_split, n - 1)
                nc.vector.tensor_tensor(val, v_sb[:, (j - 1) % 2], colp[:, :], ALU.mult)\
                    .then_inc(val_ready, 1)

            def sum_queries(j, n):
                dve.wait_ge(e_ready, n * NT + NT)
                nc.vector.reciprocal(rz[:, j % 2], zsum[:, j % 2]).then_inc(rz_ready, 1)
                dve.wait_ge(rz_ready, n + 1)
                wait(dve, acc_split, n)
                for t in range(NT):
                    if t == 0:
                        ins = nc.vector.tensor_scalar(acc, E[:, 0, :], rz[:, j % 2, 0:1], None, ALU.mult)
                    else:
                        dve.wait_ge(acc_step, n * NT + t)
                        ins = nc.vector.scalar_tensor_tensor(acc, E[:, t, :], rz[:, j % 2, t:t + 1], acc,
                                                             ALU.mult, ALU.add)
                    ins.then_inc(acc_step, 1)

            def slot(p, j):
                n = p * SLOTS + j
                has_next = not (is_last(p) and j == SLOTS - 1)
                outs = []
                if j >= NB + 2:
                    outs = [(p, j - 2 - NB, t) for t in range(NT)]
                elif j < 2 and not is_first(p):
                    outs = [(p - 1, j + NB - 2, t) for t in range(NT)]

                def some(k):
                    if outs:
                        add_out(*outs[k])

                    if is_last(p) and j == NB + 1:
                        dve.wait_ge(prep_hi, k + 1)
                        nc.vector.tensor_tensor(WT[:, LO, k], outp[:, :], WT[:, HI, k].bitcast(fp32),
                                                ALU.subtract).then_inc(prep_ready, 1)

                if is_first(p) and j < NB - 1:
                    for t in range(NT):
                        maximum(j, n, t)
                    first_low(j + 1)
                    q_low(j + 1, n + 1)
                    if j > 0:
                        values(j, n)
                    sum_queries(j, n)
                    k_low(j + 1, n + 1)
                    if j + 2 < NB:
                        first_statistics(j + 2)
                        link(inverse_deviation(rstd[:, :], mv[:, :, 1], NT))
                        apply_norm(j + 2, j + 2, norm_buf)
                    return
                if has_next:
                    q_low(j + 1, n + 1)
                some(0)
                maximum(j, n, 0)
                maximum(j, n, 1)
                some(1)
                if has_next:
                    k_low(j + 1, n + 1)
                if not (is_first(p) and j == 0):
                    values(j, n)
                some(2)
                maximum(j, n, 2)
                maximum(j, n, 3)
                some(3)
                if is_last(p) and j == SLOTS - 1:
                    inverse_deviation(m_rstd[:, 0:NT], m_mv[:, 0:NT, 1], NT).then_inc(m_norms, 1)
                sum_queries(j, n)
                if is_last(p) and j >= SLOTS - 2:
                    memory_statistics(j - (SLOTS - 2))

            def memory_statistics(b):
                dve.wait_ge(o_added, (NPAIR - 1) * NB * NT + (b + 1) * NT)
                for t in range(NT):
                    statistics(b, t, m_mv[:, b * NT + t])

            def pair(p):
                for j in range(SLOTS):
                    slot(p, j)

            first_statistics(0)
            link(inverse_deviation(rstd[:, :], mv[:, :, 1], NT))
            apply_norm(0, 0, norm_buf)
            first_low(0)
            first_statistics(1)
            q_low(0, 0)
            link(inverse_deviation(rstd[:, :], mv[:, :, 1], NT))
            k_low(0, 0)
            apply_norm(1, 1, norm_buf)
            pairs(dve, pair)

            def memory_maximum(b):
                dve.wait_ge(ms_done, (b + 1) * NT)
                wait(dve, es_ready, b * NT)
                mask_b = maskf[:, b:b + 1, :].to_broadcast([P, NT, M])
                pen_b = pen[:, b:b + 1, :].to_broadcast([P, NT, M])
                src = product_bank("ms", b)[:, 0:NT * M].rearrange("p (t m) -> p t m", t=NT)
                nc.vector.scalar_tensor_tensor(sc[:, :, :], src, MSCALE, mask_b, ALU.mult, ALU.mult)\
                    .then_inc(ms_masked, 1)
                dve.wait_ge(ms_masked, b + 1)
                link(nc.vector.tensor_tensor(sc[:, :, :], sc[:, :, :], pen_b, ALU.add))
                nc.vector.tensor_reduce(mnegm[:, :], sc[:, :, :], AX.X, ALU.max, negate=True)\
                    .then_inc(ms_max, 1)

            def memory_residual(b):
                dve.wait_ge(es_ready, (b + 1) * NT)
                link(nc.vector.reciprocal(mrz[:, :], mz[:, :]))
                link(nc.vector.tensor_scalar(mrz[:, :], mrz[:, :], valid[:, b:b + 1], None, ALU.mult))
                for t in range(NT):
                    dve.wait_ge(read_done, b * NT + t + 1)
                    nc.vector.scalar_tensor_tensor(x_res[:, b, t], turn_bank("r", b, t)[:, :], mrz[:, t:t + 1],
                                                   x_res[:, b, t], ALU.mult, ALU.add).then_inc(x2_ready, 1)
                    if t >= 1:
                        dve.wait_ge(x2_ready, b * NT + t)
                        statistics(b, t - 1, mv[:, t - 1])
                dve.wait_ge(x2_ready, (b + 1) * NT)
                statistics(b, NT - 1, mv[:, NT - 1])
                link(inverse_deviation(rstd[:, :], mv[:, :, 1], NT))

            def router(b):
                dve.wait_ge(xa_copied, (b + 1) * NT)
                wait(dve, htr_done, b)
                nc.vector.tensor_tensor(z[:, :, :], xa[:, :, ER:XW],
                                        rb1b[:, :].unsqueeze(1).to_broadcast([P, NT, RH]), ALU.add)\
                    .then_inc(z_ready, 1)
                dve.wait_ge(ez_ready, b + 1)
                link(nc.vector.tensor_scalar(ez[:, :, :], ez[:, :, :], 1.0, None, ALU.add))
                link(nc.vector.reciprocal(ez[:, :, :], ez[:, :, :]))
                nc.vector.tensor_tensor(z[:, :, :], z[:, :, :], ez[:, :, :], ALU.mult).then_inc(h_ready, 1)
                dve.wait_ge(lg_done, b + 1)
                nc.vector.tensor_tensor(lg[:, :, :],
                                        turn_bank("l", b)[:, 0:NT * NE].rearrange("p (t e) -> p t e", t=NT),
                                        rbgb[:, :].unsqueeze(1).to_broadcast([P, NT, NE]), ALU.add)\
                    .then_inc(lg_ready, 1)
                dve.wait_ge(lg_ready, b + 1)
                for t in range(NT):
                    ins = nc.vector.max(out=top[:, t, :], in_=lg[:, t, :])
                    ins.then_inc(dve_chain, 1)
                    chain[0] += 1
                dve.wait_ge(dve_chain, chain[0])
                nc.vector.tensor_tensor(dd[:, :], top[:, :, 1], top[:, :, 0], ALU.subtract)\
                    .then_inc(dd_ready, 1)
                for t in range(NT):
                    ins = nc.vector.max_index(out=topi[:, t, :], in_max=top[:, t, :], in_values=lg[:, t, :])
                    ins.then_inc(dve_chain, 1)
                    chain[0] += 1
                dve.wait_ge(dve_chain, chain[0])
                link(nc.vector.tensor_copy(topf[:, :, :], topi[:, :, 0:2]))
                dve.wait_ge(ed_ready, b + 1)
                link(nc.vector.tensor_scalar(dd[:, :], p2[:, :], 1.0, None, ALU.add))
                link(nc.vector.reciprocal(p1[:, :], dd[:, :]))
                link(nc.vector.tensor_tensor(p2[:, :], p2[:, :], p1[:, :], ALU.mult))
                wait(dve, wxa_ready, b * NT)
                for s in range(2):
                    ins = nc.vector.tensor_tensor(
                        cf[:, s], iot[:, :].unsqueeze(1).to_broadcast([P, NT, NE]),
                        topf[:, :, s:s + 1].to_broadcast([P, NT, NE]), ALU.is_equal)
                    ins.then_inc(dve_chain, 1)
                    chain[0] += 1
                dve.wait_ge(dve_chain, chain[0])
                for s, pr in ((0, p1), (1, p2)):
                    ins = nc.vector.tensor_tensor(
                        cf[:, s], cf[:, s], pr[:, :].unsqueeze(2).to_broadcast([P, NT, NE]), ALU.mult)
                    ins.then_inc(dve_chain, 1)
                    chain[0] += 1
                dve.wait_ge(dve_chain, chain[0])
                nc.vector.tensor_tensor(cf[:, 0], cf[:, 0], cf[:, 1], ALU.add).then_inc(cf_ready, 1)

            last = NPAIR - 1
            add_out(last, NB - 2, 0)
            add_out(last, NB - 2, 1)
            values(0, NSLOT)
            add_out(last, NB - 2, 2)
            add_out(last, NB - 2, 3)
            for k in range(NK):
                dve.wait_ge(prep_hi, NK + k + 1)
                nc.vector.tensor_tensor(XAW[:, LO, k], turn_bank("xaw", k)[:, 0:XW],
                                        XAW[:, HI, k].bitcast(fp32), ALU.subtract).then_inc(prep_ready, 1)
            for t in range(NT):
                add_out(last, NB - 1, t)
            dve.wait_ge(small_loaded, 16 * 6)
            link(nc.vector.tensor_copy(maskf[:, :, :], maskb[:, :, :]))
            link(nc.vector.tensor_scalar(pen[:, :, :], maskf[:, :, :], 1.0, NEG, ALU.subtract, ALU.mult))
            link(nc.vector.tensor_reduce(valid[:, :], maskf[:, :, :], AX.X, ALU.max))
            link(nc.vector.tensor_tensor(rbgb[:, :], rbgb[:, :], gateb[:, :], ALU.add))
            memory_maximum(0)
            for a in range(NA):
                dve.wait_ge(prep_hi, 2 * NK + a + 1)
                nc.vector.tensor_tensor(BT[:, LO, a], turn_bank("bt", a)[:, :], BT[:, HI, a].bitcast(fp32),
                                        ALU.subtract).then_inc(prep_ready, 1)
            dve.wait_ge(prep_done, NPREP + 1)
            nc.vector.tensor_copy(rw2T[:, :], turn_bank("rw2")[0:RH, 0:NE]).then_inc(prep_ready, 1)
            memory_statistics(2)
            memory_statistics(3)
            inverse_deviation(m_rstd[:, NT:], m_mv[:, NT:, 1], (NB - 1) * NT).then_inc(m_norms, 1)
            memory_residual(0)
            for b in range(NB):
                more = b + 1 < NB
                apply_norm(number["x", b], b, E)
                if more:
                    memory_maximum(b + 1)
                for t in range(NT):
                    dve.wait_ge(xhi_ready, (NB + b) * NT + t + 1)
                    at = slice(t * P, (t + 1) * P)
                    nc.vector.tensor_tensor(x2T[:, LO, :, at],
                                            turn_bank("x", b, t)[:, :].rearrange("p (k n) -> p k n", k=NK),
                                            x2T[:, HI, :, at].bitcast(fp32), ALU.subtract)\
                        .then_inc(xlo_ready, 1)
                router(b)
                if more:
                    memory_residual(b + 1)
                for t in range(NT):
                    dve.wait_ge(y_mm, b * NT + t + 1)
                    dve.wait_ge(biased, b * NT + t + 1)
                    nc.vector.tensor_tensor(x_res[:, b, t], x_res[:, b, t], sps[t][:, :], ALU.add)\
                        .then_inc(y_ready, 1)


_INS = ["x", "ctx_2048", "mask_BxS2_bk0", "L0_attn_w_qkv", "L0_attn_w_o", "L0_ffn_W", "L0_ffn_bias",
        "L0_ffn_rw1", "L0_ffn_rb1", "L0_ffn_rw2", "L0_ffn_rb2", "L0_ffn_A", "L0_ffn_B", "L0_ffn_gates"]


def kernel(**inputs):
    import numpy as np
    import concourse.bacc as bacc
    from concourse.bass_utils import run_bass_kernel_spmd

    nc = bacc.Bacc("TRN2", target_bir_lowering=False, num_devices=1, dynamic_dma_scratch_size=1024)
    arrays, args = {}, []
    for name in _INS:
        a = np.ascontiguousarray(inputs[name])
        arrays[f"in_{name}"] = a
        args.append(nc.dram_tensor(f"in_{name}", a.shape, mybir.dt.from_np(a.dtype), kind="ExternalInput").ap())
    shape = inputs["x"].shape
    out = nc.dram_tensor("out_0", shape, mybir.dt.float32, kind="ExternalOutput").ap()
    decoder_layer(nc, *args, out)
    r = run_bass_kernel_spmd(nc, [arrays], core_ids=[0])
    return r.results[0]["out_0"]
```

```python
import math
from contextlib import ExitStack

import concourse.bass as bass
from concourse import mybir


def decoder_layer(nc, A_x, A_mem, A_mask, A_wqkv, A_wo, A_W, A_bias, A_rw1, A_rb1, A_rw2, A_rb2,
                  A_A, A_B, A_gates, out):
    fp32 = mybir.dt.float32
    f32r = mybir.dt.float32r
    i32 = mybir.dt.int32
    u32 = mybir.dt.uint32
    ALU = mybir.AluOpType
    ACT = mybir.ActivationFunctionType
    AX = mybir.AxisListType

    P = 128
    NB, SQ, D = A_x.shape
    NT = SQ // P
    NK = D // P
    F = A_wqkv.shape[1] // 3
    DH = P
    NH = F // DH
    NPAIR = NH // 2
    SLOTS = 2 * NB
    NSLOT = NPAIR * SLOTS
    M = A_mem.shape[1]
    NE, RANK = A_A.shape[0], A_A.shape[1]
    ER = NE * RANK
    NA = ER // P
    RH = A_rw1.shape[0]
    XW = ER + RH
    SCALE = 1.0 / math.sqrt(DH)
    MSCALE = 1.0 / math.sqrt(D)
    EPS = 1e-5
    NEG = 1e30
    HI, LO = 0, 1
    H = P // 2
    X, MEM = 0, 1

    x_view = A_x.rearrange("b (t p) d -> p b t d", p=P)
    out_view = out.rearrange("b (t p) d -> p b t d", p=P)
    wqkv_view = A_wqkv.rearrange("(k p) (c n d) -> n c p k d", p=P, c=3, d=DH)
    wo_view = A_wo.rearrange("(q j d) n -> q d j n", j=2, d=DH)

    ctx = ExitStack()
    with ctx:
        def sb(name, shape, dt=fp32):
            return ctx.enter_context(nc.sbuf_tensor(name, shape, dt))

        def sem(name):
            return ctx.enter_context(nc.semaphore(name))

        x_res = sb("x_res", [P, NB, NT, D])
        ident = sb("ident", [P, P])
        big = sb("big", [P, NB, 2 * NK * SQ], f32r)
        xT = big[:, :, :].rearrange("p b (h k n) -> p b h k n", h=2, k=NK)
        wsp = sb("wsp", [P, 2, 2, NK, 3 * DH], f32r)
        wstage = sb("wstage", [P, (NK * 3 * DH + 2 * D)])
        wq_raw = wstage[:, 0:NK * 3 * DH].rearrange("p (k c d) -> p k c d", k=NK, c=3)
        wo_raw = wstage[:, NK * 3 * DH:].rearrange("p (j n) -> p j n", j=2)
        wosp = sb("wosp", [P, 2, 2, D], f32r)
        qk = sb("qk", [P, 2, 2, 2, SQ], f32r)
        work = sb("work", [P, 4, SQ])
        v_sb = work[:, 0:2, :]
        acc = work[:, 2, :]
        val = work[:, 3, :]
        E = sb("E", [P, NT, SQ])
        lower = sb("lower", [H, SQ])
        accsp = sb("accsp", [P, SQ], f32r)
        ones = sb("ones", [P, P], f32r)
        val0 = sb("val0", [P, NB, 2, SQ], f32r)
        val1 = sb("val1", [P, 2, 2, SQ], f32r)
        negm = sb("negm", [P, 2, NT])
        zsum = sb("zsum", [P, 2, NT])
        rz = sb("rz", [P, 2, NT])
        bn = sb("bn", [P, NT, 6])
        mv = sb("mv", [P, 2, NT, 2])
        rstd = sb("rstd", [P, 2, NT])
        va = sb("va", [P, 2, NT])
        half = sb("half", [P, 2, NT], i32)
        yt = sb("yt", [P, 2, NT])
        norm_buf = sb("norm_buf", [P, NT, D])
        maskb = sb("maskb", [P, NB, M], A_mask.dtype)
        maskf = sb("maskf", [P, NB, M])
        pen = sb("pen", [P, NB, M])
        valid = sb("valid", [P, NB])
        memT = sb("memT", [P, NB, NK, M])
        sc = sb("sc", [P, NT, M])
        es = sb("es", [P, NT, M])
        mnegm = sb("mnegm", [P, NT])
        mz = sb("mz", [P, NT])
        mrz = sb("mrz", [P, NT])
        biasb = sb("biasb", [P, D])
        rb1b = sb("rb1b", [P, RH])
        rbgb = sb("rbgb", [P, NE])
        gateb = sb("gateb", [P, NE])
        rw2_raw = sb("rw2_raw", [NE, RH])
        rw2T = sb("rw2T", [RH, NE])
        iot = sb("iot", [P, NE])
        z = sb("z", [P, NT, RH])
        ez = sb("ez", [P, NT, RH])
        lg = sb("lg", [P, NT, NE])
        top = sb("top", [P, NT, 8])
        topi = sb("topi", [P, NT, 8], u32)
        topf = sb("topf", [P, NT, 2])
        dd = sb("dd", [P, NT])
        p1 = sb("p1", [P, NT])
        p2 = sb("p2", [P, NT])
        cf = sb("cf", [P, 2, NT, NE])

        WT = big[:, 0].rearrange("p (h k n) -> p h k n", h=2, k=NK)
        XAW = big[:, 1, 0:2 * NK * XW].rearrange("p (h k n) -> p h k n", h=2, k=NK)
        BT = big[:, 2, 0:2 * NA * D].rearrange("p (h a n) -> p h a n", h=2, a=NA)
        wxT = big[:, 2, 2 * NA * D:2 * NA * D + NT * 2 * ER].rearrange("p (s h n) -> p s h n", s=NT, h=2)
        x2T = big[:, 3].rearrange("p (h k n) -> p h k n", h=2, k=NK)
        W_raw = wstage[:, 0:NK * D].rearrange("p (t i) -> p t i", i=D)
        A_raw = wstage[:, 0:NA * D].rearrange("p (a i) -> p a i", i=D)
        B_raw = wstage[:, NA * D:NA * D + NK * ER].rearrange("p (t n) -> p t n", n=ER)
        rw1_raw = wstage[0:RH, NK * D:(NK + 1) * D]
        xa = wstage[:, 0:NT * XW].rearrange("p (t n) -> p t n", t=NT)
        wxa = wstage[:, NT * XW:NT * (XW + ER)].rearrange("p (t n) -> p t n", t=NT)
        x1T = work[:, 0:2, :].rearrange("p s (k n) -> p s k n", k=NK)
        hT = work[0:RH, 2, :]
        eT = work[0:M, 3, :]
        mem_raw = norm_buf[0:M]

        proj = [ctx.enter_context(nc.psum_tensor(f"proj{i}", [P, SQ], fp32)) for i in range(2)]
        sps = [ctx.enter_context(nc.psum_tensor(f"score{i}", [P, SQ], fp32)) for i in range(NT)]
        colp = ctx.enter_context(nc.psum_tensor("colp", [P, SQ], fp32))
        outp = ctx.enter_context(nc.psum_tensor("outp", [P, SQ], fp32))

        x_loaded = {b: sem(f"x_loaded{b}") for b in range(1, NB)}
        tile_loaded = [sem(f"tile_loaded{t}") for t in range(NT)]
        w_loaded = sem("w_loaded")
        wo_loaded = sem("wo_loaded")
        small_loaded = sem("small_loaded")
        mem_loaded = sem("mem_loaded")
        W_loaded = sem("W_loaded")
        tail_loaded = sem("tail_loaded")
        stored = sem("stored")
        ident_ready = sem("ident_ready")
        ones_ready = sem("ones_ready")
        dve_chain = sem("dve_chain")
        pool_chain = sem("pool_chain")
        xn_ready = sem("xn_ready")
        xtr_done = sem("xtr_done")
        xhi_ready = sem("xhi_ready")
        xlo_ready = sem("xlo_ready")
        w_hi = sem("w_hi")
        w_split = sem("w_split")
        wo_hi = sem("wo_hi")
        wo_split = sem("wo_split")
        q_proj = sem("q_proj")
        k_proj = sem("k_proj")
        v_proj = sem("v_proj")
        q_hi = sem("q_hi")
        k_hi = sem("k_hi")
        q_split = sem("q_split")
        k_split = sem("k_split")
        v_copied = sem("v_copied")
        s_done = sem("s_done")
        max_ready = sem("max_ready")
        e_ready = sem("e_ready")
        rz_ready = sem("rz_ready")
        acc_step = sem("acc_step")
        acc_moved = sem("acc_moved")
        acc_folded = sem("acc_folded")
        acc_hi = sem("acc_hi")
        acc_split = sem("acc_split")
        c_done = sem("c_done")
        val_ready = sem("val_ready")
        val_hi = sem("val_hi")
        val_split = sem("val_split")
        o_done = sem("o_done")
        o_added = sem("o_added")
        prep_done = sem("prep_done")
        prep_hi = sem("prep_hi")
        prep_ready = sem("prep_ready")
        memtr_done = sem("memtr_done")
        memT_ready = sem("memT_ready")
        x1_ready = sem("x1_ready")
        ms_done = sem("ms_done")
        ms_masked = sem("ms_masked")
        ms_max = sem("ms_max")
        es_ready = sem("es_ready")
        etr_done = sem("etr_done")
        eT_ready = sem("eT_ready")
        read_done = sem("read_done")
        x2_ready = sem("x2_ready")
        xa_done = sem("xa_done")
        xa_copied = sem("xa_copied")
        z_ready = sem("z_ready")
        ez_ready = sem("ez_ready")
        h_ready = sem("h_ready")
        htr_done = sem("htr_done")
        hT_ready = sem("hT_ready")
        lg_done = sem("lg_done")
        lg_ready = sem("lg_ready")
        cf_ready = sem("cf_ready")
        dd_ready = sem("dd_ready")
        ed_ready = sem("ed_ready")
        wxa_ready = sem("wxa_ready")
        wtr_done = sem("wtr_done")
        wx_hi = sem("wx_hi")
        wx_full = sem("wx_full")
        wx_ready = sem("wx_ready")
        biased = sem("biased")
        y_mm = sem("y_mm")
        y_ready = sem("y_ready")

        def wait(eng, semaphore, value):
            if not isinstance(value, int) or value > 0:
                eng.wait_ge(semaphore, value)

        def is_first(p):
            return isinstance(p, int) and p == 0

        NPREP = NK + NK + NA

        def is_last(p):
            return isinstance(p, int) and p == NPAIR - 1

        FIRST_ORDER = [(0, 0), (0, 1), (1, 0), (1, 1), (2, 0), (3, 0), (2, 1), (3, 1)]
        FIRST_TURNS = {2: 2, 3: 3}

        def step(p, j):
            if is_first(p) and 0 <= j < SLOTS:
                return FIRST_ORDER[j]
            return j % NB, j // NB % 2

        def pairs(eng, body):
            body(0)
            with eng.Fori(1, NPAIR - 1) as p:
                body(p)
            body(NPAIR - 1)

        NORMS = [("a", b) for b in range(NB)] + [("m", 0), ("x", 0), ("m", 1)]
        for b in range(1, NB):
            NORMS += [("m", b + 1)] * (b + 1 < NB) + [("x", b)]
        number = {what: u for u, what in enumerate(NORMS)}
        TURNS = [("m", 0, t) for t in range(NT)] + [("xaw", k) for k in range(NK)] + [("e", 0)]
        TURNS += [("r", 0, t) for t in range(NT)]
        TURNS += [("bt", a) for a in range(NA)] + [("rw2",)]
        PRODUCTS = [("ms", 0)]
        for b in range(NB):
            more = b + 1 < NB
            memory_turns = [("m", b + 1, t) for t in range(NT * more)]
            TURNS += memory_turns * (b > 0) + [("h", b), ("l", b)] + memory_turns * (b == 0)
            TURNS += [("e", b + 1)] * more + [("r", b + 1, t) for t in range(NT * more)]
            TURNS += [("w", b, t) for t in range(NT)]
            products = [("xa", b, t) for t in range(NT)]
            PRODUCTS += [("ms", b + 1)] * more + products if b > 0 else products + [("ms", b + 1)]

        def turn_bank(*what):
            return proj[TURNS.index(what) % 2]

        def product_bank(*what):
            return (colp, outp)[PRODUCTS.index(what) % 2]

        def first_bank(b, t):
            return sps[t] if b == 0 else (outp, colp, proj[1], sps[0])[t] if b == 1 \
                else (outp, colp, outp, sps[0])[t]

        def out_bank(p, b, t):
            if not is_last(p) or b == 0:
                return outp
            return LAST_BANKS[(b - 1) * NT + t]

        LAST_BANKS = [outp] + sps + [outp, sps[0], sps[1], outp, colp, sps[2], sps[3]]

        def next_weights(p, j):
            if j == 1 and not is_first(p):
                return p * 2 + 1, 1
            if j == (6 if is_first(p) else 1 + NB) and not is_last(p):
                return p * 2 + 2, 0

        def weigh(engine, t):
            return engine.tensor_tensor(wxa[:, t].rearrange("p (e r) -> p e r", r=RANK),
                                        xa[:, t, 0:ER].rearrange("p (e r) -> p e r", r=RANK),
                                        cf[:, 0, t].unsqueeze(2).to_broadcast([P, NE, RANK]), ALU.mult)

        def w_half(parity, f):
            return wsp[:, parity, f].rearrange("p k n -> p (k n)")

        block = ctx.enter_context(nc.Block())

        @block.sync
        def _(sp):
            def load_w(h):
                for c in range(3):
                    sp.dma_start(wq_raw[:, :, c, :], wqkv_view[h, c]).then_inc(w_loaded, 16)

            for t in range(NT):
                sp.dma_start(x_res[:, 0, t], x_view[:, 0, t]).then_inc(tile_loaded[t], 16)
            load_w(0)
            sp.dma_start(x_res[:, 1], x_view[:, 1]).then_inc(x_loaded[1], 16)

            def pair(p):
                sp.wait_ge(w_split, p * 2 + 1)
                load_w(p * 2 + 1)
                if is_first(p):
                    for b in range(2, NB):
                        sp.dma_start(x_res[:, b], x_view[:, b]).then_inc(x_loaded[b], 16)
                wait(sp, wo_split, p)
                sp.dma_start(wo_raw, wo_view[p]).then_inc(wo_loaded, 16)
                if is_first(p):
                    sp.dma_start(maskb[:, :, :], A_mask.partition_broadcast(P)).then_inc(small_loaded, 16)
                    sp.dma_start(biasb[:, :], A_bias.partition_broadcast(P)).then_inc(small_loaded, 16)
                    sp.dma_start(rb1b[:, :], A_rb1.partition_broadcast(P)).then_inc(small_loaded, 16)
                    sp.dma_start(rbgb[:, :], A_rb2[0:NE].partition_broadcast(P)).then_inc(small_loaded, 16)
                    sp.dma_start(gateb[:, :], A_gates.partition_broadcast(P)).then_inc(small_loaded, 16)
                    sp.dma_start(rw2_raw[:, :], A_rw2[0:NE, :]).then_inc(small_loaded, 16)
                if not is_last(p):
                    sp.wait_ge(w_split, p * 2 + 2)
                    load_w(p * 2 + 2)
                if is_first(p):
                    sp.wait_ge(xtr_done, NB * NT)
                    sp.dma_start(mem_raw, A_mem.rearrange("b m d -> m b d")).then_inc(mem_loaded, 16)

            pairs(sp, pair)
            sp.wait_ge(w_split, NH)
            sp.wait_ge(wo_split, NPAIR)
            sp.dma_start(W_raw, A_W.rearrange("(t p) i -> p t i", p=P)).then_inc(W_loaded, 16)
            sp.dma_start(rw1_raw, A_rw1).then_inc(tail_loaded, 16)
            sp.wait_ge(prep_done, NK)
            sp.dma_start(A_raw, A_A.rearrange("e r i -> (e r) i").rearrange("(a p) i -> p a i", p=P))\
                .then_inc(tail_loaded, 16)
            b_view = A_B.rearrange("e (t p) r -> t p e r", p=P)
            for t in range(D // P):
                sp.dma_start(B_raw[:, t, :].rearrange("p (e r) -> p e r", r=RANK), b_view[t])\
                    .then_inc(tail_loaded, 16)
            for b in range(NB - 1):
                sp.wait_ge(y_ready, NT * (b + 1))
                sp.dma_start(out_view[:, b], x_res[:, b]).then_inc(stored, 16)
            for t in range(NT):
                sp.wait_ge(y_ready, NT * (NB - 1) + t + 1)
                sp.dma_start(out_view[:, NB - 1, t], x_res[:, NB - 1, t]).then_inc(stored, 16)
            sp.wait_ge(stored, 16 * (NB - 1 + NT))

        @block.gpsimd
        def _(pool):
            chain = [0]

            def link(ins):
                chain[0] += 1
                ins.then_inc(pool_chain, 1)
                pool.wait_ge(pool_chain, chain[0])

            link(nc.gpsimd.memset(ident[:, :], 0.0))
            nc.gpsimd.affine_select(out=ident[:, :], in_=ident[:, :], compare_op=ALU.not_equal, fill=1.0,
                                    base=0, pattern=[[-1, P]], channel_multiplier=1).then_inc(ident_ready, 1)
            nc.gpsimd.memset(ones[:, :].bitcast(fp32), 1.0).then_inc(ones_ready, 1)
            pool.wait_ge(ones_ready, 1)
            link(nc.gpsimd.iota(iot[:, :], pattern=[[1, NE]], base=0, channel_multiplier=0,
                                allow_small_or_imprecise_dtypes=True))

            def high(dst, src):
                one = ones[0:src.shape[0], 0:1].bitcast(fp32).to_broadcast([src.shape[0], src.shape[1]])
                return nc.gpsimd.tensor_tensor(dst, src, one, ALU.mult)

            def high_w(h, parity):
                pool.wait_ge(w_loaded, h * 48 + 48)
                high(w_half(parity, HI), wstage[:, 0:NK * 3 * DH]).then_inc(w_hi, 1)

            def low_w(h, parity):
                pool.wait_ge(w_hi, h + 1)
                nc.gpsimd.tensor_tensor(w_half(parity, LO), wstage[:, 0:NK * 3 * DH],
                                        w_half(parity, HI).bitcast(fp32), ALU.subtract).then_inc(w_split, 1)

            def slot(p, j):
                n1 = p * SLOTS + j
                splits = next_weights(p, j)
                if not (is_first(p) and j == 0):
                    b, head = step(p, j - 1)
                    pool.wait_ge(acc_moved, n1)
                    nc.gpsimd.tensor_tensor(acc[0:H], acc[0:H], lower[:, :], ALU.add).then_inc(acc_folded, 1)
                    pool.wait_ge(acc_folded, n1)
                    wait(pool, c_done, n1 - 1)
                    high(accsp[0:H], acc[0:H]).then_inc(acc_hi, 1)
                    pool.wait_ge(acc_hi, n1)
                    nc.gpsimd.tensor_tensor(accsp[H:P], acc[0:H], accsp[0:H].bitcast(fp32),
                                            ALU.subtract).then_inc(acc_split, 1)
                    pool.wait_ge(acc_split, n1)
                    if splits:
                        low_w(*splits)
                    pool.wait_ge(val_ready, n1)
                    dst = val0[:, b] if head == 0 else val1[:, b % 2]
                    if head == 0:
                        wait(pool, o_done, p * (NB * NT) + (b + 1 - NB) * NT)
                    elif j == 0:
                        wait(pool, o_done, p * (NB * NT) + (b - 1 - NB) * NT)
                    else:
                        wait(pool, o_done, p * (NB * NT) + (b - 1) * NT)
                    high(dst[:, HI], val).then_inc(val_hi, 1)
                    pool.wait_ge(val_hi, n1)
                    nc.gpsimd.tensor_tensor(dst[:, LO], val, dst[:, HI].bitcast(fp32),
                                            ALU.subtract).then_inc(val_split, 1)
                if j == 3:
                    raw = wstage[:, NK * 3 * DH:]
                    hi, lo = (wosp[:, f].rearrange("p j n -> p (j n)") for f in (HI, LO))
                    pool.wait_ge(wo_hi, p + 1)
                    nc.gpsimd.tensor_tensor(lo, raw, hi.bitcast(fp32), ALU.subtract).then_inc(wo_split, 1)

            def pair(p):
                for j in range(SLOTS):
                    slot(p, j)

            low_w(0, 0)
            high_w(1, 1)
            low_w(1, 1)
            pairs(pool, pair)
            slot(NPAIR, 0)

            for b in range(NB):
                pool.wait_ge(xn_ready, NT * (number["x", b] + 1))
                for t in range(NT):
                    nc.gpsimd.tensor_tensor(x_res[:, b, t], x_res[:, b, t], biasb[:, :], ALU.add)\
                        .then_inc(biased, 1)
                for t in range(NT if b < NB - 1 else 0):
                    pool.wait_ge(cf_ready, b + 1)
                    weigh(nc.gpsimd, t).then_inc(wxa_ready, 1)
                for t in range(NT):
                    pool.wait_ge(wx_full, b * NT + t + 1)
                    nc.gpsimd.tensor_tensor(wxT[:, t, LO], wxa[:, t], wxT[:, t, HI].bitcast(fp32),
                                            ALU.subtract).then_inc(wx_ready, 1)

        @block.tensor
        def _(pe):
            def halves(out_ap, lhsT, rhs, start, stop):
                nc.tensor.matmul(out_ap, lhsT(HI), rhs(HI), start=start, stop=False)
                nc.tensor.matmul(out_ap, lhsT(HI), rhs(LO), start=False, stop=False)
                return nc.tensor.matmul(out_ap, lhsT(LO), rhs(HI), start=False, stop=stop)

            def turn_tile(bank, src):
                for k in range(NK):
                    mm = nc.tensor.transpose(bank[:, k * P:(k + 1) * P], src[:, k * P:(k + 1) * P], ident[:, :])
                return mm

            def first_turn(b, t):
                pe.wait_ge(xn_ready, b * NT + t + 1)
                if b > 0 and t == 3:
                    pe.wait_ge(e_ready, (0, 0, 2, 3)[b] * NT + 1)
                elif b > 1 and t == 1:
                    pe.wait_ge(val_ready, b - 1)
                elif b > 1:
                    pe.wait_ge(xlo_ready, b * NT + t // 2)
                turn_tile(first_bank(b, t), norm_buf[:, t, :]).then_inc(xtr_done, 1)

            def project(c, b, parity, bank):
                for k in range(NK):
                    mm = halves(proj[bank][:, :],
                                lambda f: wsp[:, parity, f, k, c * DH:(c + 1) * DH],
                                lambda f: xT[:, b, f, k, :], k == 0, k == NK - 1)
                return mm

            def q_project(p, j, n):
                b, head = step(p, j)
                if b == 0:
                    pe.wait_ge(w_split, p * 2 + (head if j < SLOTS else 2) + 1)
                if is_first(p) and j < SLOTS and head == 0:
                    pe.wait_ge(xlo_ready, (b + 1) * NT)
                if is_first(p) and j == 1:
                    pe.wait_ge(v_copied, n)
                else:
                    wait(pe, k_split, n)
                project(0, b, head, (n_parity(j - 1) * 3) % 2).then_inc(q_proj, 1)

            def n_parity(j):
                return j % 2

            def k_project(p, j, n):
                wait(pe, v_copied, n - 1)
                project(1, *step(p, j), (n_parity(j - 1) * 3 + 1) % 2).then_inc(k_proj, 1)

            def v_project(p, j, n, has_next):
                if is_first(p) and j == 0:
                    pe.wait_ge(k_split, n + 1)
                elif has_next:
                    pe.wait_ge(q_split, n + 2)
                project(2, *step(p, j), (n_parity(j) * 3 + 2) % 2).then_inc(v_proj, 1)

            def scores(j, n, t):
                if t == 0:
                    pe.wait_ge(q_split, n + 1)
                    pe.wait_ge(k_split, n + 1)
                wait(pe, e_ready, n * NT + (t + 1 - NT))
                halves(sps[t][:, :], lambda f: qk[:, j % 2, 0, f, t * P:(t + 1) * P],
                       lambda f: qk[:, j % 2, 1, f, :], True, True).then_inc(s_done, 1)

            def column_sums(n):
                pe.wait_ge(acc_split, n)
                wait(pe, val_ready, n - 1)
                nc.tensor.matmul(colp[:, :], ones[:, :], accsp[:, :], start=True, stop=True)\
                    .then_inc(c_done, 1)

            def out_tile(p, b, t):
                if t == 0:
                    pe.wait_ge(val_split, p * SLOTS + NB + b + 1)
                    if b == 0:
                        pe.wait_ge(wo_split, p + 1)
                bank = out_bank(p, b, t)
                before = p * (NB * NT) + b * NT + t
                i = (b - 1) * NT + t
                if is_last(p) and 1 <= i <= NT:
                    pe.wait_ge(e_ready, (NSLOT - 1) * NT + i)
                elif is_last(p) and bank is colp:
                    pe.wait_ge(ms_masked, 1)
                elif is_last(p) and i > NT:
                    used = max(u for u in range(i) if LAST_BANKS[u] is bank)
                    pe.wait_ge(o_added, before - i + used + 1)
                else:
                    wait(pe, o_added, before)
                if is_last(p) and b == 0 and t == 0:
                    pe.wait_ge(prep_ready, NK)
                halves(bank[:, :], lambda f: val0[:, b, f, t * P:(t + 1) * P],
                       lambda f: wosp[:, f, 0, :], True, False)
                halves(bank[:, :], lambda f: val1[:, b % 2, f, t * P:(t + 1) * P],
                       lambda f: wosp[:, f, 1, :], False, True).then_inc(o_done, 1)

            def slot(p, j):
                n = p * SLOTS + j
                has_next = not (is_last(p) and j == SLOTS - 1)
                outs = []
                if j >= NB + 2:
                    outs = [(p, j - 2 - NB, t) for t in range(NT)]
                elif j < 2 and not is_first(p):
                    outs = [(p - 1, j + NB - 2, t) for t in range(NT)]

                def some(k):
                    if outs:
                        out_tile(*outs[k])
                    if is_last(p) and j == NB:
                        turn_memory(k)
                    if is_last(p) and j == NB + 1:
                        turn_W(k)

                if is_first(p) and j == 0:
                    for t in range(NT):
                        scores(j, n, t)
                    v_project(p, j, n, True)
                    for t in range(NT):
                        first_turn(1, t)
                    q_project(p, j + 1, n + 1)
                    pe.wait_ge(xlo_ready, NT + 3)
                    k_project(p, j + 1, n + 1)
                    return
                if not has_next:
                    for t in range(NT):
                        scores(j, n, t)
                    v_project(p, j, n, has_next)
                    for t in range(NT):
                        if t == 3:
                            column_sums(n)
                        out_tile(*outs[t])
                    return

                def turn(t):
                    if is_first(p) and j in FIRST_TURNS:
                        first_turn(FIRST_TURNS[j], t)

                q_project(p, j + 1, n + 1)
                some(0)
                turn(0)
                scores(j, n, 0)
                scores(j, n, 1)
                some(1)
                turn(1)
                k_project(p, j + 1, n + 1)
                turn(2)
                some(2)
                scores(j, n, 2)
                scores(j, n, 3)
                if outs:
                    column_sums(n)
                turn(3)
                v_project(p, j, n, True)
                if not outs:
                    if is_first(p) and j in FIRST_TURNS:
                        pe.wait_ge(xlo_ready, FIRST_TURNS[j] * NT + 2)
                    column_sums(n)
                some(3)

            def turn_memory(b):
                if b == 0:
                    pe.wait_ge(mem_loaded, 16)
                    pe.wait_ge(o_added, (NPAIR - 1) * NB * NT)
                else:
                    pe.wait_ge(memT_ready, b)
                for k in range(NK):
                    mm = nc.tensor.matmul(outp[:, k * M:(k + 1) * M], mem_raw[:, b, k * P:(k + 1) * P],
                                          ident[0:M, 0:M], start=True, stop=True)
                mm.then_inc(memtr_done, 1)

            def turn_W(k):
                if k == 0:
                    pe.wait_ge(W_loaded, 16)
                    pe.wait_ge(memT_ready, NB)
                else:
                    pe.wait_ge(prep_ready, k)
                for t in range(D // P):
                    mm = nc.tensor.transpose(outp[:, t * P:(t + 1) * P], W_raw[:, t, k * P:(k + 1) * P],
                                             ident[:, :])
                mm.then_inc(prep_done, 1)

            def pair(p):
                for j in range(SLOTS):
                    slot(p, j)

            pe.wait_ge(ident_ready, 1)
            for t in range(NT):
                first_turn(0, t)
            pe.wait_ge(ones_ready, 1)
            pe.wait_ge(xlo_ready, NT)
            q_project(0, 0, 0)
            k_project(0, 0, 0)
            pairs(pe, pair)

            def released(what):
                kind, b, t = (*what, 0, 0)[:3]
                return {"xaw": (prep_ready, NK + b + 1), "bt": (prep_ready, 2 * NK + b + 1),
                        "rw2": (prep_ready, NPREP + 1), "m": (x1_ready, b * NT + t + 1),
                        "h": (hT_ready, b + 1),
                        "l": (lg_ready, b + 1), "e": (eT_ready, b + 1), "r": (x2_ready, b * NT + t + 1),
                        "w": (wx_full, b * NT + t + 1), "ms": (ms_masked, b + 1),
                        "xa": (xa_copied, b * NT + t + 1)}[kind]

            first_release = [(v_copied, NSLOT - 1), (v_copied, NSLOT)]

            def take_turn(*what):
                i = TURNS.index(what)
                pe.wait_ge(*(released(TURNS[i - 2]) if i >= 2 else first_release[i]))
                return turn_bank(*what)

            def take_product(*what):
                i = PRODUCTS.index(what)
                if i == 0:
                    pe.wait_ge(val_ready, NSLOT)
                elif i <= 2:
                    pe.wait_ge(o_added, NPAIR * NB * NT - NT + i)
                else:
                    pe.wait_ge(*released(PRODUCTS[i - 2]))
                return product_bank(*what)

            def turned(kind, b, t):
                pe.wait_ge(xn_ready, number[kind, b] * NT + t + 1)
                if kind == "x":
                    if b == 0:
                        used = max(u for u in range(len(LAST_BANKS)) if LAST_BANKS[u] is sps[t])
                        pe.wait_ge(o_added, (NPAIR - 1) * NB * NT + NT + used + 1)
                    else:
                        pe.wait_ge(y_ready, (b - 1) * NT + t + 1)
                    bank = sps[t]
                else:
                    bank = take_turn(kind, b, t)
                turn_tile(bank, E[:, t, :]).then_inc(xtr_done, 1)

            def turn_xaw(k):
                bank = take_turn("xaw", k)
                for a in range(NA):
                    nc.tensor.transpose(bank[:, a * P:(a + 1) * P], A_raw[:, a, k * P:(k + 1) * P], ident[:, :])
                nc.tensor.matmul(bank[:, ER:XW], rw1_raw[:, k * P:(k + 1) * P], ident[0:RH, 0:RH],
                                 start=True, stop=True).then_inc(prep_done, 1)

            def turn_bt(a):
                bank = take_turn("bt", a)
                for t in range(D // P):
                    mm = nc.tensor.transpose(bank[:, t * P:(t + 1) * P], B_raw[:, t, a * P:(a + 1) * P],
                                             ident[:, :])
                mm.then_inc(prep_done, 1)

            def memory_scores(b, between):
                for t in range(NT + 1):
                    if t < NT:
                        turned("m", b, t)
                    between(t)
                    if t >= 1:
                        bank = take_product("ms", b) if t == 1 else product_bank("ms", b)
                        pe.wait_ge(x1_ready, b * NT + t)
                        for k in range(NK):
                            mm = nc.tensor.matmul(bank[:, (t - 1) * M:t * M], x1T[:, (t - 1) % 2, k, :],
                                                  memT[:, b, k, :], start=(k == 0), stop=(k == NK - 1))
                        mm.then_inc(ms_done, 1)

            def turn_probabilities(b):
                pe.wait_ge(es_ready, (b + 1) * NT)
                bank = take_turn("e", b)
                for t in range(NT):
                    mm = nc.tensor.matmul(bank[0:M, t * P:(t + 1) * P], es[:, t, :], ident[:, :],
                                          start=True, stop=True)
                mm.then_inc(etr_done, 1)

            def readout(b, t):
                pe.wait_ge(eT_ready, b + 1)
                nc.tensor.matmul(take_turn("r", b, t)[:, :], eT[:, t * P:(t + 1) * P], mem_raw[:, b, :],
                                 start=True, stop=True).then_inc(read_done, 1)

            def first_product(b):
                for t in range(NT + 1):
                    if 0 < t < NT:
                        turned("x", b, t)
                    if t >= 1:
                        pe.wait_ge(xlo_ready, (NB + b) * NT + t)
                        bank = take_product("xa", b, t - 1)
                        for k in range(NK):
                            mm = halves(bank[:, 0:XW], lambda f: x2T[:, f, k, (t - 1) * P:t * P],
                                        lambda f: XAW[:, f, k, :], k == 0, k == NK - 1)
                        mm.then_inc(xa_done, 1)

            def turn_h(b):
                pe.wait_ge(h_ready, b + 1)
                bank = take_turn("h", b)
                for t in range(NT):
                    mm = nc.tensor.matmul(bank[0:RH, t * P:(t + 1) * P], z[:, t, :], ident[:, :],
                                          start=True, stop=True)
                mm.then_inc(htr_done, 1)

            def logits(b):
                pe.wait_ge(hT_ready, b + 1)
                bank = take_turn("l", b)
                for t in range(NT):
                    mm = nc.tensor.matmul(bank[:, t * NE:(t + 1) * NE], hT[:, t * P:(t + 1) * P],
                                          rw2T[:, :], start=True, stop=True)
                mm.then_inc(lg_done, 1)

            def base(b, t, of=range(NK)):
                pe.wait_ge(xlo_ready, (NB + b) * NT + t + 1)
                for k in of:
                    halves(sps[t][:, :], lambda f: x2T[:, f, k, t * P:(t + 1) * P],
                           lambda f: WT[:, f, k, :], k == 0, False)

            def turn_weighed(b, t):
                pe.wait_ge(wxa_ready, b * NT + t + 1)
                bank = take_turn("w", b, t)
                for a in range(NA):
                    mm = nc.tensor.transpose(bank[:, a * P:(a + 1) * P], wxa[:, t, a * P:(a + 1) * P],
                                             ident[:, :])
                mm.then_inc(wtr_done, 1)

            def delta(b, t):
                pe.wait_ge(wx_ready, b * NT + t + 1)
                for a in range(NA):
                    mm = halves(sps[t][:, :], lambda f: wxT[:, t, f, a * P:(a + 1) * P],
                                lambda f: BT[:, f, a, :], False, a == NA - 1)
                mm.then_inc(y_mm, 1)

            last = NPAIR - 1
            def beside_first_memory(t):
                if t == 1:
                    column_sums(NSLOT)
                    out_tile(last, NB - 2, 1)

            out_tile(last, NB - 2, 0)
            memory_scores(0, beside_first_memory)
            pe.wait_ge(tail_loaded, 16 * (2 + D // P))
            turn_xaw(0)
            turn_xaw(1)
            out_tile(last, NB - 2, 2)
            turn_xaw(2)
            turn_xaw(3)
            turn_probabilities(0)
            out_tile(last, NB - 2, 3)
            for t in range(NT):
                readout(0, t)
            for t in range(NT):
                out_tile(last, NB - 1, t)
            for a in range(NA):
                turn_bt(a)
            for b in range(NB):
                more = b + 1 < NB
                if more and b > 0:
                    memory_scores(b + 1, lambda t: turned("x", b, 0) if t == NT else None)
                if b == 0:
                    turned("x", 0, 0)
                    pe.wait_ge(prep_ready, 2 * NK)
                first_product(b)
                if b == 0:
                    pe.wait_ge(small_loaded, 16 * 6)
                    nc.tensor.matmul(take_turn("rw2")[0:RH, 0:NE], rw2_raw[:, :], ident[0:NE, 0:NE],
                                     start=True, stop=True).then_inc(prep_done, 1)
                base(b, 0)
                base(b, 1)
                turn_h(b)
                base(b, 2, [0, 1])
                if b == 0:
                    pe.wait_ge(prep_ready, NPREP + 1)
                logits(b)
                base(b, 2, [2, 3])
                if b == 0:
                    memory_scores(1, lambda t: None)
                if b == 0:
                    base(b, 3)
                if more:
                    turn_probabilities(b + 1)
                if b > 0:
                    base(b, 3, [0])
                for t in range(NT):
                    if more:
                        readout(b + 1, t)
                    if b > 0 and t > 0:
                        base(b, 3, [t])
                for t in range(NT):
                    turn_weighed(b, t)
                for t in range(NT):
                    if b == NB - 2 and t == NT - 1:
                        turned("x", NB - 1, 0)
                    delta(b, t)

        @block.scalar
        def _(act):
            def first_high(b, t):
                act.wait_ge(xtr_done, b * NT + t + 1)
                nc.scalar.activation(xT[:, b, HI, :, t * P:(t + 1) * P],
                                     first_bank(b, t)[:, :].rearrange("p (k n) -> p k n", k=NK), ACT.Copy)\
                    .then_inc(xhi_ready, 1)

            def q_high(j, n):
                act.wait_ge(q_proj, n + 1)
                wait(act, s_done, n * NT - NT)
                nc.scalar.activation(qk[:, j % 2, 0, HI], proj[((j - 1) % 2 * 3) % 2][:, :], ACT.Copy,
                                     scale=SCALE).then_inc(q_hi, 1)

            def k_high(j, n):
                act.wait_ge(k_proj, n + 1)
                nc.scalar.activation(qk[:, j % 2, 1, HI], proj[((j - 1) % 2 * 3 + 1) % 2][:, :], ACT.Copy)\
                    .then_inc(k_hi, 1)

            def exponentials(j, n, t):
                act.wait_ge(max_ready, n * NT + t + 1)
                wait(act, acc_step, n * NT + (t + 1 - NT))
                nc.scalar.activation(E[:, t, :], sps[t][:, :], ACT.Exp, bias=negm[:, j % 2, t:t + 1],
                                     accum_out=zsum[:, j % 2, t:t + 1]).then_inc(e_ready, 1)

            def slot(p, j):
                n = p * SLOTS + j
                has_next = not (is_last(p) and j == SLOTS - 1)
                splits = next_weights(p, j)
                if splits:
                    h, parity = splits
                    act.wait_ge(w_loaded, h * 48 + 48)
                    act.wait_ge(v_proj, 6 if is_first(p) else p * SLOTS + (0 if j == 1 else NB))
                    nc.scalar.activation(w_half(parity, HI), wstage[:, 0:NK * 3 * DH], ACT.Copy)\
                        .then_inc(w_hi, 1)
                if j == 3:
                    act.wait_ge(wo_loaded, p * 16 + 16)
                    wait(act, o_done, p * (NB * NT))
                    nc.scalar.activation(wosp[:, HI].rearrange("p j n -> p (j n)"), wstage[:, NK * 3 * DH:],
                                         ACT.Copy).then_inc(wo_hi, 1)
                if is_first(p) and j == 0:
                    for t in range(NT - 1):
                        exponentials(j, n, t)
                    copy_values(j, n)
                    exponentials(j, n, NT - 1)
                    for t in range(NT):
                        first_high(1, t)
                    q_high(j + 1, n + 1)
                    k_high(j + 1, n + 1)
                    return
                if not has_next:
                    move_sums(n)
                    for t in range(NT):
                        exponentials(j, n, t)
                    copy_values(j, n)
                    move_sums(NSLOT)
                    return
                q_high(j + 1, n + 1)
                move_sums(n)
                prepare(p, j, 0)
                turned_high(p, j, 0)
                exponentials(j, n, 0)
                exponentials(j, n, 1)
                prepare(p, j, 1)
                turned_high(p, j, 1)
                k_high(j + 1, n + 1)
                turned_high(p, j, 2)
                prepare(p, j, 2)
                exponentials(j, n, 2)
                turned_high(p, j, 3)
                exponentials(j, n, 3)
                copy_values(j, n)
                prepare(p, j, 3)

            def move_sums(n):
                act.wait_ge(acc_step, n * NT)
                wait(act, acc_folded, n - 1)
                nc.scalar.activation(lower[:, :], acc[H:P], ACT.Copy).then_inc(acc_moved, 1)

            def copy_values(j, n):
                act.wait_ge(v_proj, n + 1)
                wait(act, val_ready, n - 1)
                nc.scalar.activation(v_sb[:, j % 2], proj[(j % 2 * 3 + 2) % 2][:, :], ACT.Copy)\
                    .then_inc(v_copied, 1)

            def turned_high(p, j, t):
                if is_first(p) and j in FIRST_TURNS:
                    first_high(FIRST_TURNS[j], t)

            def prepare(p, j, k):
                if is_last(p) and j == NB:
                    act.wait_ge(memtr_done, k + 1)
                    nc.scalar.activation(memT[:, k].rearrange("p k m -> p (k m)"), outp[:, 0:NK * M],
                                         ACT.Copy).then_inc(memT_ready, 1)
                if is_last(p) and j == NB + 1:
                    act.wait_ge(prep_done, k + 1)
                    act.wait_ge(v_proj, NSLOT - NB + 1)
                    nc.scalar.activation(WT[:, HI, k], outp[:, :], ACT.Copy).then_inc(prep_hi, 1)

            def pair(p):
                for j in range(SLOTS):
                    slot(p, j)

            act.wait_ge(w_loaded, 48)
            nc.scalar.activation(w_half(0, HI), wstage[:, 0:NK * 3 * DH], ACT.Copy).then_inc(w_hi, 1)
            for t in range(NT):
                first_high(0, t)
            q_high(0, 0)
            k_high(0, 0)
            pairs(act, pair)

            def memory_tiles(b, of=range(NT)):
                for t in of:
                    act.wait_ge(xtr_done, number["m", b] * NT + t + 1)
                    wait(act, ms_done, b * NT + t - 1)
                    if b == 0 and t < 2:
                        act.wait_ge(val_ready, NSLOT - 1 + t)
                    nc.scalar.activation(x1T[:, t % 2], turn_bank("m", b, t)[:, :].rearrange(
                        "p (k n) -> p k n", k=NK), ACT.Copy).then_inc(x1_ready, 1)

            def memory_exponentials(b):
                act.wait_ge(ms_max, b + 1)
                for t in range(NT):
                    nc.scalar.activation(es[:, t, :], sc[:, t, :], ACT.Exp, bias=mnegm[:, t:t + 1],
                                         accum_out=mz[:, t:t + 1]).then_inc(es_ready, 1)

            def memory_turned(b):
                act.wait_ge(etr_done, b + 1)
                if b == 0:
                    act.wait_ge(val_split, NSLOT)
                nc.scalar.activation(eT, turn_bank("e", b)[0:M, :], ACT.Copy).then_inc(eT_ready, 1)

            def high(b, t):
                act.wait_ge(xtr_done, number["x", b] * NT + t + 1)
                wait(act, y_mm, (b - 1) * NT + t + 1)
                nc.scalar.activation(x2T[:, HI, :, t * P:(t + 1) * P], sps[t][:, :].rearrange(
                    "p (k n) -> p k n", k=NK), ACT.Copy).then_inc(xhi_ready, 1)

            def copy_xa(b, t):
                act.wait_ge(xa_done, b * NT + t + 1)
                wait(act, wxa_ready, (b - 1) * NT + t + 1)
                nc.scalar.activation(xa[:, t, :], product_bank("xa", b, t)[:, 0:XW], ACT.Copy)\
                    .then_inc(xa_copied, 1)

            def xaw_high(k):
                act.wait_ge(prep_done, NK + k + 1)
                nc.scalar.activation(XAW[:, HI, k], turn_bank("xaw", k)[:, 0:XW], ACT.Copy).then_inc(prep_hi, 1)

            memory_tiles(0)
            xaw_high(0)
            xaw_high(1)
            memory_exponentials(0)
            xaw_high(2)
            xaw_high(3)
            memory_turned(0)
            for a in range(NA):
                act.wait_ge(prep_done, 2 * NK + a + 1)
                nc.scalar.activation(BT[:, HI, a], turn_bank("bt", a)[:, :], ACT.Copy).then_inc(prep_hi, 1)
            for b in range(NB):
                more = b + 1 < NB
                if more and b > 0:
                    memory_tiles(b + 1)
                high(b, 0)
                high(b, 1)
                if more and b > 0:
                    memory_exponentials(b + 1)
                copy_xa(b, 0)
                high(b, 2)
                copy_xa(b, 1)
                high(b, 3)
                copy_xa(b, 2)
                copy_xa(b, 3)
                act.wait_ge(z_ready, b + 1)
                nc.scalar.activation(ez[:, :, :], z[:, :, :], ACT.Exp, scale=-1.0).then_inc(ez_ready, 1)
                act.wait_ge(htr_done, b + 1)
                nc.scalar.activation(hT, turn_bank("h", b)[0:RH, :], ACT.Copy).then_inc(hT_ready, 1)
                if b == 0:
                    memory_tiles(1, [0, 1])
                act.wait_ge(dd_ready, b + 1)
                nc.scalar.activation(p2[:, :], dd[:, :], ACT.Exp).then_inc(ed_ready, 1)
                if b == 0:
                    memory_tiles(1, [2, 3])
                    memory_exponentials(1)
                if more:
                    memory_turned(b + 1)
                for t in range(NT):
                    act.wait_ge(wtr_done, b * NT + t + 1)
                    wait(act, y_mm, (b - 1) * NT + t + 1)
                    nc.scalar.activation(wxT[:, t, HI], turn_bank("w", b, t)[:, 0:ER], ACT.Copy)\
                        .then_inc(wx_hi, 1)
                    nc.scalar.activation(wxa[:, t], turn_bank("w", b, t)[:, 0:ER], ACT.Copy)\
                        .then_inc(wx_full, 1)

        @block.vector
        def _(dve):
            chain = [0]

            def link(ins):
                chain[0] += 1
                ins.then_inc(dve_chain, 1)
                dve.wait_ge(dve_chain, chain[0])

            def statistics(b, t, out_mv):
                link(nc.vector.bn_stats(bn[:, t], x_res[:, b, t]))
                nc.vector.bn_aggr(out_mv, bn[:, t]).then_inc(dve_chain, 1)
                chain[0] += 1

            def inverse_deviation(start, end=None, between=None):
                of = slice(start, start + 1 if end is None else end)
                y, v, h, w = rstd[:, of], va[:, of], half[:, of], yt[:, of]
                steps = [0]

                def follow(ins):
                    chain[0] += 1
                    ins.then_inc(dve_chain, 1)
                    done = chain[0]
                    if between:
                        between(steps[0])
                    steps[0] += 1
                    dve.wait_ge(dve_chain, done)

                dve.wait_ge(dve_chain, chain[0])
                follow(nc.vector.tensor_scalar(v, mv[:, of, :, 1], EPS, None, ALU.add))
                follow(nc.vector.tensor_scalar(h, v.bitcast(i32), 1, None, ALU.logical_shift_right))
                follow(nc.vector.tensor_scalar(y.bitcast(i32), h, -1.0, float(0x5F3759DF), ALU.mult, ALU.add))
                for step in range(3):
                    follow(nc.vector.tensor_tensor(w, y, y, ALU.mult))
                    follow(nc.vector.scalar_tensor_tensor(w, w, -0.5, v, ALU.mult, ALU.mult))
                    follow(nc.vector.scalar_tensor_tensor(y, w, 1.5, y, ALU.add, ALU.mult))

            def apply_norm(kind, b, dst, of=range(NT)):
                for t in of:
                    wait(dve, xtr_done, (number[kind, b] - 1) * NT + t + 1)
                    of = MEM if kind == "m" else X
                    mean, inverse = mv[:, of, t, 0:1], rstd[:, of, t:t + 1]
                    nc.vector.tensor_scalar(dst[:, t, :], x_res[:, b, t], mean, inverse,
                                            ALU.subtract, ALU.mult).then_inc(xn_ready, 1)

            def first_statistics(b):
                if b > 0:
                    dve.wait_ge(x_loaded[b], 16)
                for t in range(NT):
                    if b == 0:
                        dve.wait_ge(tile_loaded[t], 16)
                    statistics(b, t, mv[:, X, t])

            def first_low(b, t):
                dve.wait_ge(xhi_ready, b * NT + t + 1)
                at = slice(t * P, (t + 1) * P)
                nc.vector.tensor_tensor(xT[:, b, LO, :, at],
                                        first_bank(b, t)[:, :].rearrange("p (k n) -> p k n", k=NK),
                                        xT[:, b, HI, :, at].bitcast(fp32), ALU.subtract)\
                    .then_inc(xlo_ready, 1)

            def q_low(j, n):
                dve.wait_ge(q_hi, n + 1)
                nc.vector.scalar_tensor_tensor(qk[:, j % 2, 0, LO], proj[((j - 1) % 2 * 3) % 2][:, :], SCALE,
                                               qk[:, j % 2, 0, HI].bitcast(fp32), ALU.mult, ALU.subtract)\
                    .then_inc(q_split, 1)

            def k_low(j, n):
                dve.wait_ge(k_hi, n + 1)
                nc.vector.tensor_tensor(qk[:, j % 2, 1, LO], proj[((j - 1) % 2 * 3 + 1) % 2][:, :],
                                        qk[:, j % 2, 1, HI].bitcast(fp32), ALU.subtract)\
                    .then_inc(k_split, 1)

            def maximum(j, n, t):
                dve.wait_ge(s_done, n * NT + t + 1)
                nc.vector.tensor_reduce(negm[:, j % 2, t:t + 1], sps[t][:, :], AX.X, ALU.max, negate=True)\
                    .then_inc(max_ready, 1)

            def add_out(p, b, t):
                dve.wait_ge(o_done, p * (NB * NT) + b * NT + t + 1)
                nc.vector.tensor_tensor(x_res[:, b, t], x_res[:, b, t], out_bank(p, b, t)[:, :], ALU.add)\
                    .then_inc(o_added, 1)

            def values(j, n):
                dve.wait_ge(c_done, n)
                dve.wait_ge(v_copied, n)
                wait(dve, val_split, n - 1)
                nc.vector.tensor_tensor(val, v_sb[:, (j - 1) % 2], colp[:, :], ALU.mult)\
                    .then_inc(val_ready, 1)

            def sum_queries(j, n):
                dve.wait_ge(e_ready, n * NT + NT)
                nc.vector.reciprocal(rz[:, j % 2], zsum[:, j % 2]).then_inc(rz_ready, 1)
                dve.wait_ge(rz_ready, n + 1)
                wait(dve, acc_split, n)
                for t in range(NT):
                    if t == 0:
                        ins = nc.vector.tensor_scalar(acc, E[:, 0, :], rz[:, j % 2, 0:1], None, ALU.mult)
                    else:
                        dve.wait_ge(acc_step, n * NT + t)
                        ins = nc.vector.scalar_tensor_tensor(acc, E[:, t, :], rz[:, j % 2, t:t + 1], acc,
                                                             ALU.mult, ALU.add)
                    ins.then_inc(acc_step, 1)

            def slot(p, j):
                n = p * SLOTS + j
                has_next = not (is_last(p) and j == SLOTS - 1)
                outs = []
                if j >= NB + 2:
                    outs = [(p, j - 2 - NB, t) for t in range(NT)]
                elif j < 2 and not is_first(p):
                    outs = [(p - 1, j + NB - 2, t) for t in range(NT)]

                def some(k):
                    if outs:
                        add_out(*outs[k])
                    if is_last(p) and j == NB + 2 and k > 0:
                        memory_statistics(0, [k - 1])
                    if is_first(p) and (j, k) in ((1, 1), (1, 3), (2, 0), (2, 1)):
                        t = (j - 1) * 2 + (k // 2 if j == 1 else k)
                        dve.wait_ge(x_loaded[3], 16)
                        statistics(3, t, mv[:, X, t])
                    if is_last(p) and j == NB + 1:
                        dve.wait_ge(prep_hi, k + 1)
                        nc.vector.tensor_tensor(WT[:, LO, k], outp[:, :], WT[:, HI, k].bitcast(fp32),
                                                ALU.subtract).then_inc(prep_ready, 1)

                if is_first(p) and j == 0:
                    apply_norm("a", 1, norm_buf)
                    for t in range(NT):
                        maximum(j, n, t)
                    for t in range(NT):
                        first_low(1, t)
                    sum_queries(j, n)
                    q_low(j + 1, n + 1)
                    k_low(j + 1, n + 1)
                    first_statistics(2)
                    inverse_deviation(X)
                    apply_norm("a", 2, norm_buf)
                    return

                if not has_next:
                    inverse_deviation(MEM, between=lambda i: maximum(j, n, i // 2) if i in (0, 2, 4, 6) else None)
                    values(j, n)
                    sum_queries(j, n)
                    return

                def low(t):
                    if is_first(p) and j in FIRST_TURNS:
                        first_low(FIRST_TURNS[j], t)

                q_low(j + 1, n + 1)
                some(0)
                low(0)
                maximum(j, n, 0)
                maximum(j, n, 1)
                some(1)
                low(1)
                k_low(j + 1, n + 1)
                low(2)
                some(2)
                maximum(j, n, 2)
                maximum(j, n, 3)
                low(3)
                if is_first(p) and j == 2:
                    inverse_deviation(X)
                    apply_norm("a", 3, norm_buf)
                values(j, n)
                some(3)
                if is_last(p) and j == NB + 2:
                    memory_statistics(0, [NT - 1])
                sum_queries(j, n)
                if is_first(p) and j == SLOTS - 3:
                    mask_constants()

            def mask_constants():
                dve.wait_ge(small_loaded, 16 * 6)
                link(nc.vector.tensor_copy(maskf[:, :, :], maskb[:, :, :]))
                link(nc.vector.tensor_scalar(pen[:, :, :], maskf[:, :, :], 1.0, NEG, ALU.subtract, ALU.mult))
                link(nc.vector.tensor_reduce(valid[:, :], maskf[:, :, :], AX.X, ALU.max))
                link(nc.vector.tensor_tensor(rbgb[:, :], rbgb[:, :], gateb[:, :], ALU.add))

            def memory_statistics(b, of=range(NT)):
                for t in of:
                    dve.wait_ge(o_added, (NPAIR - 1) * NB * NT + b * NT + t + 1)
                    statistics(b, t, mv[:, MEM, t])

            def pair(p):
                for j in range(SLOTS):
                    slot(p, j)

            first_statistics(0)
            inverse_deviation(X)
            apply_norm("a", 0, norm_buf)
            for t in range(NT):
                first_low(0, t)
            first_statistics(1)
            q_low(0, 0)
            k_low(0, 0)
            inverse_deviation(X)
            pairs(dve, pair)

            def memory_maximum(b):
                dve.wait_ge(ms_done, (b + 1) * NT)
                wait(dve, es_ready, b * NT)
                mask_b = maskf[:, b:b + 1, :].to_broadcast([P, NT, M])
                pen_b = pen[:, b:b + 1, :].to_broadcast([P, NT, M])
                src = product_bank("ms", b)[:, 0:NT * M].rearrange("p (t m) -> p t m", t=NT)
                nc.vector.scalar_tensor_tensor(sc[:, :, :], src, MSCALE, mask_b, ALU.mult, ALU.mult)\
                    .then_inc(ms_masked, 1)
                dve.wait_ge(ms_masked, b + 1)
                link(nc.vector.tensor_tensor(sc[:, :, :], sc[:, :, :], pen_b, ALU.add))
                nc.vector.tensor_reduce(mnegm[:, :], sc[:, :, :], AX.X, ALU.max, negate=True)\
                    .then_inc(ms_max, 1)

            def memory_residual(b):
                dve.wait_ge(es_ready, (b + 1) * NT)
                link(nc.vector.reciprocal(mrz[:, :], mz[:, :]))
                link(nc.vector.tensor_scalar(mrz[:, :], mrz[:, :], valid[:, b:b + 1], None, ALU.mult))
                for t in range(NT):
                    dve.wait_ge(read_done, b * NT + t + 1)
                    nc.vector.scalar_tensor_tensor(x_res[:, b, t], turn_bank("r", b, t)[:, :], mrz[:, t:t + 1],
                                                   x_res[:, b, t], ALU.mult, ALU.add).then_inc(x2_ready, 1)
                    if t > 0:
                        residual_statistics(b, t - 1)
                residual_statistics(b, NT - 1)

            def residual_statistics(b, t):
                dve.wait_ge(x2_ready, b * NT + t + 1)
                statistics(b, t, mv[:, X, t])

            def router(b):
                dve.wait_ge(xa_copied, (b + 1) * NT)
                wait(dve, htr_done, b)
                nc.vector.tensor_tensor(z[:, :, :], xa[:, :, ER:XW],
                                        rb1b[:, :].unsqueeze(1).to_broadcast([P, NT, RH]), ALU.add)\
                    .then_inc(z_ready, 1)
                dve.wait_ge(ez_ready, b + 1)
                link(nc.vector.tensor_scalar(ez[:, :, :], ez[:, :, :], 1.0, None, ALU.add))
                link(nc.vector.reciprocal(ez[:, :, :], ez[:, :, :]))
                nc.vector.tensor_tensor(z[:, :, :], z[:, :, :], ez[:, :, :], ALU.mult).then_inc(h_ready, 1)

            def choose(b):
                dve.wait_ge(lg_done, b + 1)
                nc.vector.tensor_tensor(lg[:, :, :],
                                        turn_bank("l", b)[:, 0:NT * NE].rearrange("p (t e) -> p t e", t=NT),
                                        rbgb[:, :].unsqueeze(1).to_broadcast([P, NT, NE]), ALU.add)\
                    .then_inc(lg_ready, 1)
                dve.wait_ge(lg_ready, b + 1)
                for t in range(NT):
                    ins = nc.vector.max(out=top[:, t, :], in_=lg[:, t, :])
                    ins.then_inc(dve_chain, 1)
                    chain[0] += 1
                dve.wait_ge(dve_chain, chain[0])
                nc.vector.tensor_tensor(dd[:, :], top[:, :, 1], top[:, :, 0], ALU.subtract)\
                    .then_inc(dd_ready, 1)
                for t in range(NT):
                    ins = nc.vector.max_index(out=topi[:, t, :], in_max=top[:, t, :], in_values=lg[:, t, :])
                    ins.then_inc(dve_chain, 1)
                    chain[0] += 1
                dve.wait_ge(dve_chain, chain[0])
                link(nc.vector.tensor_copy(topf[:, :, :], topi[:, :, 0:2]))
                dve.wait_ge(ed_ready, b + 1)
                link(nc.vector.tensor_scalar(dd[:, :], p2[:, :], 1.0, None, ALU.add))
                link(nc.vector.reciprocal(p1[:, :], dd[:, :]))
                link(nc.vector.tensor_tensor(p2[:, :], p2[:, :], p1[:, :], ALU.mult))
                wait(dve, wxa_ready, b * NT)
                for s in range(2):
                    ins = nc.vector.tensor_tensor(
                        cf[:, s], iot[:, :].unsqueeze(1).to_broadcast([P, NT, NE]),
                        topf[:, :, s:s + 1].to_broadcast([P, NT, NE]), ALU.is_equal)
                    ins.then_inc(dve_chain, 1)
                    chain[0] += 1
                dve.wait_ge(dve_chain, chain[0])
                for s, pr in ((0, p1), (1, p2)):
                    ins = nc.vector.tensor_tensor(
                        cf[:, s], cf[:, s], pr[:, :].unsqueeze(2).to_broadcast([P, NT, NE]), ALU.mult)
                    ins.then_inc(dve_chain, 1)
                    chain[0] += 1
                dve.wait_ge(dve_chain, chain[0])
                nc.vector.tensor_tensor(cf[:, 0], cf[:, 0], cf[:, 1], ALU.add).then_inc(cf_ready, 1)
                if b == NB - 1:
                    dve.wait_ge(cf_ready, b + 1)
                    for t in range(NT):
                        dve.wait_ge(wx_ready, (b - 1) * NT + t + 1)
                        weigh(nc.vector, t).then_inc(wxa_ready, 1)

            def subtract_high(dst, src):
                return nc.vector.tensor_tensor(dst[LO], src, dst[HI].bitcast(fp32), ALU.subtract)

            def xaw_low(k):
                dve.wait_ge(prep_hi, NK + k + 1)
                subtract_high((XAW[:, HI, k], XAW[:, LO, k]), turn_bank("xaw", k)[:, 0:XW])\
                    .then_inc(prep_ready, 1)

            def low(b, t):
                dve.wait_ge(xhi_ready, (NB + b) * NT + t + 1)
                at = slice(t * P, (t + 1) * P)
                subtract_high((x2T[:, HI, :, at], x2T[:, LO, :, at]),
                              sps[t][:, :].rearrange("p (k n) -> p k n", k=NK)).then_inc(xlo_ready, 1)

            last = NPAIR - 1
            dve.wait_ge(acc_step, NSLOT * NT)
            apply_norm("m", 0, E)
            add_out(last, 1, 0)
            add_out(last, 1, 1)
            values(NSLOT, NSLOT)
            for b, t in ((1, 2), (1, 3), (2, 0), (2, 1)):
                add_out(last, b, t)
            memory_maximum(0)
            xaw_low(0)
            xaw_low(1)
            add_out(last, NB - 2, 2)
            xaw_low(2)
            xaw_low(3)
            add_out(last, NB - 2, 3)
            memory_residual(0)
            inverse_deviation(X)
            apply_norm("x", 0, E, [0, 1])
            add_out(last, NB - 1, 0)
            apply_norm("x", 0, E, [2])
            for b in range(NB):
                more = b + 1 < NB
                if 0 < b < NB - 1:
                    apply_norm("x", b, E)
                for t in range(NT):
                    low(b, t)
                    if b == 0:
                        if t == 0:
                            add_out(last, NB - 1, 1)
                            add_out(last, NB - 1, 2)
                        if t == 1:
                            apply_norm("x", 0, E, [3])
                            add_out(last, NB - 1, 3)
                        if t < NA:
                            dve.wait_ge(prep_hi, 2 * NK + t + 1)
                            subtract_high((BT[:, HI, t], BT[:, LO, t]), turn_bank("bt", t)[:, :])\
                                .then_inc(prep_ready, 1)
                        memory_statistics(1, [t])
                    elif t == 0 and more:
                        memory_maximum(b + 1)
                if b == 0:
                    dve.wait_ge(prep_done, NPREP + 1)
                    nc.vector.tensor_copy(rw2T[:, :], turn_bank("rw2")[0:RH, 0:NE]).then_inc(prep_ready, 1)
                router(b)
                if b == 0:
                    inverse_deviation(MEM)
                    apply_norm("m", 1, E)
                if b + 2 < NB:
                    memory_statistics(b + 2)
                choose(b)
                if b == 0:
                    memory_maximum(1)
                def outputs(t):
                    dve.wait_ge(y_mm, b * NT + t + 1)
                    dve.wait_ge(biased, b * NT + t + 1)
                    nc.vector.tensor_tensor(x_res[:, b, t], x_res[:, b, t], sps[t][:, :], ALU.add)\
                        .then_inc(y_ready, 1)

                if more:
                    memory_residual(b + 1)
                if b + 2 < NB:
                    inverse_deviation(X, MEM + 1)
                    apply_norm("m", b + 2, E)
                elif more:
                    inverse_deviation(X, between=lambda i: outputs(i // 5 - 1) if i in (5, 10) else None)
                    apply_norm("x", b + 1, E)
                for t in range(2 if b == NB - 2 else 0, NT):
                    outputs(t)


_INS = ["x", "ctx_2048", "mask_BxS2_bk0", "L0_attn_w_qkv", "L0_attn_w_o", "L0_ffn_W", "L0_ffn_bias",
        "L0_ffn_rw1", "L0_ffn_rb1", "L0_ffn_rw2", "L0_ffn_rb2", "L0_ffn_A", "L0_ffn_B", "L0_ffn_gates"]


def kernel(**inputs):
    import numpy as np
    import concourse.bacc as bacc
    from concourse.bass_utils import run_bass_kernel_spmd

    nc = bacc.Bacc("TRN2", target_bir_lowering=False, num_devices=1, dynamic_dma_scratch_size=1024)
    arrays, args = {}, []
    for name in _INS:
        a = np.ascontiguousarray(inputs[name])
        arrays[f"in_{name}"] = a
        args.append(nc.dram_tensor(f"in_{name}", a.shape, mybir.dt.from_np(a.dtype), kind="ExternalInput").ap())
    shape = inputs["x"].shape
    out = nc.dram_tensor("out_0", shape, mybir.dt.float32, kind="ExternalOutput").ap()
    decoder_layer(nc, *args, out)
    r = run_bass_kernel_spmd(nc, [arrays], core_ids=[0])
    return r.results[0]["out_0"]
```
